# Optimizing a Trainium2 kernel written in Bass

```python
import numpy as np
import jax
import jax.numpy as jnp

def _softmax(x, axis=-1):
    return jax.nn.softmax(x, axis=axis)

def _gelu(x):
    return jax.nn.gelu(x, approximate=True)

def _silu(x):
    return jax.nn.silu(x)

def _sigmoid(x):
    return jax.nn.sigmoid(x)

def _layernorm(x, axis=-1, eps=1e-05):
    m = jnp.mean(x, axis=axis, keepdims=True)
    v = jnp.var(x, axis=axis, keepdims=True)
    return (x - m) / jnp.sqrt(v + eps)

def _scatter_add(tgt, idx, src, axis=0):
    return tgt.at[idx].add(src)

def _segment_sum(src, seg, n):
    return jax.ops.segment_sum(src, seg, n)
kernel_name = 'mk_xattn_ffn_d1_seqx_r4_ef840a'

def setup_inputs(seed: int=0):
    np.random.seed(seed)
    _w = jnp.asarray

    def _rec_inputs():
        import jax
        import jax.numpy as jnp
        _rk = jax.random.key(seed)
        x = 7.22e-05 + 1 * jax.random.normal(jax.random.fold_in(_rk, 1), (16, 128, 512), jnp.float32)
        _lenS = 128 - jax.random.randint(jax.random.fold_in(_rk, 7), (16,), 0, max(1, 128 // 4) + 1, jnp.int32)
        _lenS2 = 128 - jax.random.randint(jax.random.fold_in(_rk, 8), (16,), 0, max(1, 128 // 4) + 1, jnp.int32)
        _ctx_512P = jax.random.normal(jax.random.fold_in(_rk, 11), (16, 16, 128), jnp.float32)
        _ctx_512c = jax.random.dirichlet(jax.random.fold_in(_rk, 511), 0.3 * jnp.ones((16,), jnp.float32), (16, 128))
        _ctx_512t = jnp.einsum('bsk,bkd->bsd', _ctx_512c, _ctx_512P)
        _ctx_512t = _ctx_512t * jax.lax.rsqrt(jnp.mean(jnp.square(_ctx_512t)) + 1e-12) * 0.953939
        ctx_512 = -0.000514642 + 1.00011 * (_ctx_512t + 0.3 * jax.random.normal(jax.random.fold_in(_rk, 611), (16, 128, 128), jnp.float32))
        return (x, ctx_512)
    x, ctx_512 = _rec_inputs()

    def _L0_xattn_setup():
        import jax, jax.numpy as jnp
        import numpy as np
        N_HEADS = 16
        N_KV_HEADS = 4
        ROPE_THETA = 10000.0
        EPS = 1e-05

        def _rms_norm(x, w):
            var = jnp.mean(x * x, axis=-1, keepdims=True)
            return x * jax.lax.rsqrt(var + EPS) * w

        def _rope_sin_cos(T, head_dim, dtype):
            inv_freq = 1.0 / ROPE_THETA ** (jnp.arange(0, head_dim, 2, dtype=jnp.float32) / head_dim)
            t = jnp.arange(T, dtype=jnp.float32)
            freqs = jnp.outer(t, inv_freq)
            emb = jnp.concatenate([freqs, freqs], -1)
            return (jnp.sin(emb).astype(dtype)[None, None], jnp.cos(emb).astype(dtype)[None, None])

        def _rotate_half(x):
            h = x.shape[-1] // 2
            x1, x2 = (x[..., :h], x[..., h:])
            return jnp.concatenate([-x2, x1], axis=-1)
        key = jax.random.key(seed)
        ks = jax.random.split(key, 6)
        B, T, C = (2, 512, 512)
        Ckv = C // N_HEADS * N_KV_HEADS
        return {'q': jax.random.normal(ks[0], (B, T, C), jnp.float32), 'k': jax.random.normal(ks[1], (B, T, Ckv), jnp.float32), 'v': jax.random.normal(ks[2], (B, T, Ckv), jnp.float32), 'q_norm_w': jnp.ones((C,), jnp.float32), 'k_norm_w': jnp.ones((Ckv,), jnp.float32), 'w_out': jax.random.normal(ks[3], (C, C), jnp.float32) * C ** (-0.5)}
    _L0_xattn_all = _L0_xattn_setup()
    _L0_xattn_in = {k: v for k, v in _L0_xattn_all.items() if k in ('q_norm_w', 'k_norm_w', 'w_out')}
    del _L0_xattn_all

    def _L0_ffn_setup():
        import jax, jax.numpy as jnp
        import numpy as np
        BLOCK = 64

        def dequant4bit(q, scale):
            return (q.astype(jnp.float32) - 7.5) * jnp.repeat(scale, BLOCK, axis=1)
        key = jax.random.key(seed)
        ks = jax.random.split(key, 11)
        B, S, D, H, R = (4, 512, 512, 2048, 16)
        return {'x1': jax.random.normal(ks[0], (B, S, D), jnp.float32), 'w_up_q': jax.random.randint(ks[1], (H, D), 0, 16, dtype=jnp.int32), 'w_up_scale': jax.random.uniform(ks[2], (H, D // BLOCK), jnp.float32) * 0.02, 'b_up': jax.random.normal(ks[3], (H,), jnp.float32) * 0.01, 'w_up_lora_a': jax.random.normal(ks[4], (D, R), jnp.float32) * 0.02, 'w_up_lora_b': jax.random.normal(ks[5], (R, H), jnp.float32) * 0.02, 'w_down_q': jax.random.randint(ks[6], (D, H), 0, 16, dtype=jnp.int32), 'w_down_scale': jax.random.uniform(ks[7], (D, H // BLOCK), jnp.float32) * 0.02, 'b_down': jax.random.normal(ks[8], (D,), jnp.float32) * 0.01, 'w_down_lora_a': jax.random.normal(ks[9], (H, R), jnp.float32) * 0.02, 'w_down_lora_b': jax.random.normal(ks[10], (R, D), jnp.float32) * 0.02}
    _L0_ffn_all = _L0_ffn_setup()
    _L0_ffn_in = {k: v for k, v in _L0_ffn_all.items() if k in ('w_up_q', 'w_up_scale', 'b_up', 'w_up_lora_a', 'w_up_lora_b', 'w_down_q', 'w_down_scale', 'b_down', 'w_down_lora_a', 'w_down_lora_b')}
    del _L0_ffn_all
    return {'x': x, 'ctx_512': ctx_512, 'L0_xattn_q_norm_w': _L0_xattn_in['q_norm_w'], 'L0_xattn_k_norm_w': _L0_xattn_in['k_norm_w'], 'L0_xattn_w_out': _L0_xattn_in['w_out'], 'L0_ffn_w_up_q': _L0_ffn_in['w_up_q'], 'L0_ffn_w_up_scale': _L0_ffn_in['w_up_scale'], 'L0_ffn_b_up': _L0_ffn_in['b_up'], 'L0_ffn_w_up_lora_a': _L0_ffn_in['w_up_lora_a'], 'L0_ffn_w_up_lora_b': _L0_ffn_in['w_up_lora_b'], 'L0_ffn_w_down_q': _L0_ffn_in['w_down_q'], 'L0_ffn_w_down_scale': _L0_ffn_in['w_down_scale'], 'L0_ffn_b_down': _L0_ffn_in['b_down'], 'L0_ffn_w_down_lora_a': _L0_ffn_in['w_down_lora_a'], 'L0_ffn_w_down_lora_b': _L0_ffn_in['w_down_lora_b']}

def reference(x, ctx_512, L0_xattn_q_norm_w, L0_xattn_k_norm_w, L0_xattn_w_out, L0_ffn_w_up_q, L0_ffn_w_up_scale, L0_ffn_b_up, L0_ffn_w_up_lora_a, L0_ffn_w_up_lora_b, L0_ffn_w_down_q, L0_ffn_w_down_scale, L0_ffn_b_down, L0_ffn_w_down_lora_a, L0_ffn_w_down_lora_b):
    import jax
    import jax.numpy as jnp

    def _L0_xattn_ref(q, k, v, q_norm_w, k_norm_w, w_out):
        import jax, jax.numpy as jnp
        import numpy as np
        N_HEADS = 16
        N_KV_HEADS = 4
        ROPE_THETA = 10000.0
        EPS = 1e-05

        def _rms_norm(x, w):
            var = jnp.mean(x * x, axis=-1, keepdims=True)
            return x * jax.lax.rsqrt(var + EPS) * w

        def _rope_sin_cos(T, head_dim, dtype):
            inv_freq = 1.0 / ROPE_THETA ** (jnp.arange(0, head_dim, 2, dtype=jnp.float32) / head_dim)
            t = jnp.arange(T, dtype=jnp.float32)
            freqs = jnp.outer(t, inv_freq)
            emb = jnp.concatenate([freqs, freqs], -1)
            return (jnp.sin(emb).astype(dtype)[None, None], jnp.cos(emb).astype(dtype)[None, None])

        def _rotate_half(x):
            h = x.shape[-1] // 2
            x1, x2 = (x[..., :h], x[..., h:])
            return jnp.concatenate([-x2, x1], axis=-1)
        B, T, C = q.shape
        hd = C // N_HEADS
        g = N_HEADS // N_KV_HEADS
        q = _rms_norm(q, q_norm_w)
        k = _rms_norm(k, k_norm_w)
        q = q.reshape(B, T, N_HEADS, hd).transpose(0, 2, 1, 3)
        k = k.reshape(B, T, N_KV_HEADS, hd).transpose(0, 2, 1, 3)
        v = v.reshape(B, T, N_KV_HEADS, hd).transpose(0, 2, 1, 3)
        sin, cos = _rope_sin_cos(T, hd, q.dtype)
        q = q * cos + _rotate_half(q) * sin
        k = k * cos + _rotate_half(k) * sin
        qg = q.reshape(B, N_KV_HEADS, g, T, hd)
        scale = 1.0 / jnp.sqrt(jnp.asarray(hd, q.dtype))
        scores = jnp.einsum('bgnqd,bgkd->bgnqk', qg, k) * scale
        causal = jnp.tril(jnp.ones((T, T), bool))
        scores = jnp.where(causal, scores, jnp.asarray(-1e+30, scores.dtype))
        attn = jax.nn.softmax(scores, axis=-1)
        out = jnp.einsum('bgnqk,bgkd->bgnqd', attn, v)
        out = out.reshape(B, N_HEADS, T, hd).transpose(0, 2, 1, 3).reshape(B, T, C)
        return out @ w_out.T

    def _L0_ffn_ref(x1, w_up_q, w_up_scale, b_up, w_up_lora_a, w_up_lora_b, w_down_q, w_down_scale, b_down, w_down_lora_a, w_down_lora_b):
        import jax, jax.numpy as jnp
        import numpy as np
        BLOCK = 64

        def dequant4bit(q, scale):
            return (q.astype(jnp.float32) - 7.5) * jnp.repeat(scale, BLOCK, axis=1)
        w_up = dequant4bit(w_up_q, w_up_scale).T
        y1 = x1 @ w_up + b_up + x1 @ w_up_lora_a @ w_up_lora_b
        x2 = jax.nn.relu(y1)
        w_down = dequant4bit(w_down_q, w_down_scale).T
        y2 = x2 @ w_down + b_down + x2 @ w_down_lora_a @ w_down_lora_b
        return y2
    x = x + _L0_xattn_ref(_layernorm(x, axis=-1), ctx_512, ctx_512, L0_xattn_q_norm_w, L0_xattn_k_norm_w, L0_xattn_w_out)
    x = x + _L0_ffn_ref(_layernorm(x, axis=-1), L0_ffn_w_up_q, L0_ffn_w_up_scale, L0_ffn_b_up, L0_ffn_w_up_lora_a, L0_ffn_w_up_lora_b, L0_ffn_w_down_q, L0_ffn_w_down_scale, L0_ffn_b_down, L0_ffn_w_down_lora_a, L0_ffn_w_down_lora_b)
    return x

_drawn_inputs = setup_inputs


def setup_inputs(seed=0):
    import zlib

    import numpy as np

    out = dict(_drawn_inputs(seed))
    spreads = {'L0_xattn_q_norm_w': (1.0, 0.2), 'L0_xattn_k_norm_w': (1.0, 0.2)}
    factors = {'L0_ffn_b_up': 7.881, 'L0_ffn_b_down': 8.0}
    for name, (base, spread) in spreads.items():
        noise = np.random.default_rng([zlib.crc32(name.encode()), seed]).standard_normal(out[name].shape)
        drawn = base * np.exp(spread * noise) if base else spread * noise
        out[name] = jnp.asarray(drawn.astype(out[name].dtype))
    for name, factor in factors.items():
        out[name] = (out[name] * factor).astype(out[name].dtype)
    return out
```

```python
from contextlib import ExitStack

import concourse.bass as bass
import numpy as np
from concourse import mybir

F32 = mybir.dt.float32
F32R = mybir.dt.float32r
F16 = mybir.dt.float16
I32 = mybir.dt.int32
ALU = mybir.AluOpType
ACT = mybir.ActivationFunctionType
AXX = mybir.AxisListType.X

P = 128
EPS = 1e-5
XN_SCALE = 1024.0
W_TOP, X2_TOP = 2.0 ** 13, 2.0 ** 14
BIG = 1e30

BPB = 4
SLOTS = 32
BASE = (0, 6, 12, 19)
R_STATS, R_CENTRE, R_ROPE, R_TURN = 0, 1, 2, 3
R_SCORES = (4, 5)
R_PT = (7, 8)
R_PV, R_PROJ, R_NORM2 = 9, 10, 11
TURN2 = (17, 19, 26, 31)


def build(nc, x, ctx, qw, kw, wo, wuq, wus, bu, wua, wub, wdq, wds, bd, wda, wdb,
          cos_t, sin_t, causal, ident_d, out):
    B, T, C = x.shape
    CK = ctx.shape[2]
    HD, NG = 32, 4
    NN = C // HD // NG
    H = wuq.shape[0]
    R = wua.shape[1]
    KC, HC = C // P, H // P
    NBLK = B // BPB
    QB = 64
    SC = float(np.float32(1.0) / np.sqrt(np.float32(HD)))
    assert T == P and CK == P and NBLK == 4 and HC == 16 and KC == 4 and NN == 4

    with ExitStack() as es:
        def sb(name, shape, dt=F32):
            return es.enter_context(nc.sbuf_tensor(name, shape, dt))

        def sem(name):
            return es.enter_context(nc.semaphore(name))

        wu_hi, wu_lo = sb("wu_hi", [P, KC, H], F16), sb("wu_lo", [P, KC, H], F16)
        wd_hi, wd_lo = sb("wd_hi", [P, HC, C], F16), sb("wd_lo", [P, HC, C], F16)
        wo_hi, wo_lo = sb("wo_hi", [P, NN, C], F32R), sb("wo_lo", [P, NN, C], F32R)
        xnT_hi, xnT_lo = sb("xnT_hi", [P, KC, BPB * P], F16), sb("xnT_lo", [P, KC, BPB * P], F16)
        big = sb("big", [P, 8192])
        x2_hi = big[:, 0:4096].bitcast(F16).rearrange("p (h t) -> p h t", h=HC)
        x2_lo = big[:, 4096:8192].bitcast(F16).rearrange("p (h t) -> p h t", h=HC)
        stage = big[:, 0:4096].rearrange("p (b j c) -> p b j c", b=2, j=4)
        stage_i = big[:, 0:4096].bitcast(I32).rearrange("p (b j c) -> p b j c", b=2, j=4)
        b_up_lora = big[0:R, 4096:6144]
        a_dnT = big[0:R, 6144:8192]
        a_upT, b_dn_lora = sb("a_upT", [R, C]), sb("b_dn_lora", [R, C])
        relu = sb("relu", [P, 2, BPB * P])
        xt = sb("xt", [P, BPB, C])
        x1 = sb("x1", [P, BPB, C])
        y = sb("y", [P, BPB, C])
        kvt = sb("kvt", [P, BPB, CK])
        cw, sw = sb("cw", [P, C]), sb("sw", [P, C])
        cwk, swk = sb("cwk", [P, CK]), sb("swk", [P, CK])
        mask, ident = sb("mask", [P, P]), sb("ident", [P, P])
        cos_s, sin_s = sb("cos_s", [P, HD]), sb("sin_s", [P, HD])
        bd_bc = sb("bd_bc", [P, C])
        xc = sb("xc", [P, C])
        t_cos, t_sin, q = sb("t_cos", [P, C]), sb("t_sin", [P, C]), sb("q", [P, C])
        k_cos, k_sin, k_sum, k = (sb(s, [P, CK]) for s in ("k_cos", "k_sin", "k_sum", "k"))
        sq_junk = sb("sq_junk", [P, CK])
        qT_hi, qT_lo = sb("qT_hi", [P, NN, P], F32R), sb("qT_lo", [P, NN, P], F32R)
        kD_hi, kD_lo = sb("kD_hi", [P, NG, P], F32R), sb("kD_lo", [P, NG, P], F32R)
        pr = sb("pr", [P, NN, NG, P])
        prT = sb("prT", [P, NG, NN, P])
        a_nat = prT[:, 0, 0:3, :].rearrange("p a b -> p (a b)")[:, 0:(KC + HC) * R]
        oT_hi, oT_lo = sb("oT_hi", [P, NN, P], F32R), sb("oT_lo", [P, NN, P], F32R)
        xn2 = sb("xn2", [P, 2, C])
        stats, stats2 = sb("stats", [P, 2, 6]), sb("stats2", [P, 2, 6])
        spare = sb("spare", [P, 1])
        mv, mv2 = sb("mv", [P, 2, 2]), sb("mv2", [P, 2, 2])
        ssq = sb("ssq", [P, 2])
        arg, inv = sb("arg", [P, 2, 2]), sb("inv", [P, 2, 2])
        arg2, inv2 = sb("arg2", [P, 2]), sb("inv2", [P, 2])
        minus_half = sb("minus_half", [P, 2])
        nmax = sb("nmax", [P, 2, NN * NG])
        rsum, rinv = sb("rsum", [P, 2, NN * NG]), sb("rinv", [P, 2, NN * NG])
        s_up, s_dn = sb("s_up", [P, HC, C // QB]), sb("s_dn", [P, KC, H // QB])
        b_up = sb("b_up", [P, HC])
        tops, tops_all = sb("tops", [P, 8]), sb("tops_all", [P, 8])
        tmp = sb("tmp", [P, 16])
        kap = sb("kap", [P, 4])
        su, sd = sb("su", [P, 1]), sb("sd", [P, 1])

        def bank(name):
            return es.enter_context(nc.psum_tensor(name, [P, 512], F32))
        ff = [bank("ff0"), bank("ff1")]
        sbk = [bank("sb0"), bank("sb1")]
        tb = [bank("tb0"), bank("tb1")]
        pvb, prb = bank("pvb"), bank("prb")

        norm_w_in = sem("norm_w_in")
        consts_in, scales_in, wout_in = sem("consts_in"), sem("scales_in"), sem("wout_in")
        wq_in = [sem("wq_in0"), sem("wq_in1")]
        x_in = [sem(f"x_in{i}") for i in range(BPB)]
        kv_in = [sem(f"kv_in{i}") for i in range(BPB)]
        y_free = [sem(f"y_free{i}") for i in range(BPB)]
        tops_zero, tops_ready, tops_reduced = sem("tops_zero"), sem("tops_ready"), sem("tops_reduced")
        scale_steps, scales_ready = sem("scale_steps"), sem("scales_ready")
        tables_ready, pool_consts, diag_zero = sem("tables_ready"), sem("pool_consts"), sem("diag_zero")
        a_turned, a_copied = sem("a_turned"), sem("a_copied")
        wo_ordered = sem("wo_ordered")
        wo_turned, wo_high, wo_low = sem("wo_turned"), sem("wo_high"), sem("wo_low")
        deq_v, deq_g, deq_g1 = sem("deq_v"), sem("deq_g"), sem("deq_g1")
        w_turned, w_high, w_low = sem("w_turned"), sem("w_high"), sem("w_low")
        x_stats, x_moments, ctx_sq = sem("x_stats"), sem("x_moments"), sem("ctx_sq")
        norm_args, norms = sem("norm_args"), sem("norms")
        x_centred, q_cos, q_sin, q_ready = sem("x_centred"), sem("q_cos"), sem("q_sin"), sem("q_ready")
        k_parts, k_summed, k_ready = sem("k_parts"), sem("k_summed"), sem("k_ready")
        q_turned, k_turned = sem("q_turned"), sem("k_turned")
        q_high, q_low, k_high, k_low = sem("q_high"), sem("q_low"), sem("k_high"), sem("k_low")
        scores, masked, row_max = sem("scores"), sem("masked"), sem("row_max")
        exps, inv_sums, probs = sem("exps"), sem("inv_sums"), sem("probs")
        probs_turned, probsT = sem("probs_turned"), sem("probsT")
        heads_out, o_high, o_low = sem("heads_out"), sem("o_high"), sem("o_low")
        projected, x1_ready = sem("projected"), sem("x1_ready")
        x1_stats, x1_moments, arg2_ready, norm2 = sem("x1_stats"), sem("x1_moments"), sem("arg2_ready"), sem("norm2")
        xn2_ready, xn2_turned, xn_high, xn_low = sem("xn2_ready"), sem("xn2_turned"), sem("xn_high"), sem("xn_low")
        up_done, relu_done, x2_high, x2_low = sem("up_done"), sem("relu_done"), sem("x2_high"), sem("x2_low")
        down_done, down_read, y_base = sem("down_done"), sem("down_read"), sem("y_base")

        wuq_v = wuq.rearrange("(g j p) c -> g p j c", p=P, j=4)
        wdq_v = wdq.rearrange("(j p) (g c) -> g p j c", p=P, c=512)
        out_v = out
        wo_nat = y

        def after(eng, s, value):
            if not isinstance(value, int) or value > 0:
                eng.wait_ge(s, value)

        def halves(v, swap):
            v = v.rearrange("p (h s d) -> p h s d", s=2, d=HD // 2)
            return v[:, :, ::-1, :] if swap else v

        def scale_of(t):
            g, j = divmod(t, 4)
            v = s_up[:, t, :] if g < 4 else s_dn[:, j, 8 * (g - 4):8 * (g - 4) + 8]
            return v.unsqueeze(2).broadcast_to([P, 8, QB])

        block = es.enter_context(nc.Block())

        @block.sync
        def _(sp):
            def load_batch(A, c):
                after(sp, x1_ready, 4 * A - 3 + c)
                sp.dma_start(xt[:, c, :], x[4 * A + c]).then_inc(x_in[c], 16)
                after(sp, heads_out, 4 * A - 3 + c)
                sp.dma_start(kvt[:, c, :], ctx[4 * A + c]).then_inc(kv_in[c], 16)

            def load_group(g):
                if g >= 2:
                    after(sp, w_turned, 4 * (g - 1))
                src = wuq_v[g] if g < 4 else wdq_v[g - 4]
                sp.dma_start(stage_i[:, g % 2], src).then_inc(wq_in[g % 2], 16)

            load_batch(0, 0)
            load_batch(0, 1)
            load_group(0)
            sp.dma_start(pr[:].rearrange("p n g t -> p n (g t)"), wo.rearrange("(j p) c -> p j c", p=P)).then_inc(wout_in, 16)
            load_group(1)
            load_group(2)
            load_batch(0, 2)
            load_group(3)
            load_batch(0, 3)
            for g in range(4, 8):
                load_group(g)
            with sp.Fori(0, NBLK - 1) as i:
                for c in range(BPB):
                    load_batch(i + 1, c)

        @block.gpsimd
        def _(pool):
            for src, dst in ((bd, bd_bc), (qw, cw), (kw, cwk)):
                n = src.shape[0]
                pool.dma_start(dst[:], src.rearrange("(a n) -> a n", a=1).broadcast_to([P, n])).then_inc(norm_w_in, 16)
            for src, dst in ((qw, sw), (kw, swk)):
                sv = src.rearrange("(a h s d) -> a h s d", a=1, s=2, d=HD // 2)
                dv = dst[:].rearrange("p (h s d) -> p h s d", s=2, d=HD // 2)
                n = src.shape[0] // HD
                for s in range(2):
                    pool.dma_start(dv[:, :, s, :], sv[:, :, 1 - s, :].broadcast_to([P, n, HD // 2])).then_inc(norm_w_in, 16)
            pool.memset(minus_half[:], -0.5).then_inc(pool_consts, 1)
            for t in (kD_hi, kD_lo):
                pool.memset(t[:].bitcast(F32), 0.0).then_inc(diag_zero, 1)

            pool.wait_ge(norm_w_in, 16 * 7)
            pool.wait_ge(consts_in, 16 * 4)
            for dst, tab in ((cw, cos_s), (sw, sin_s), (cwk, cos_s), (swk, sin_s)):
                v = dst[:].rearrange("p (h d) -> p h d", d=HD)
                pool.tensor_tensor(v, v, tab[:].unsqueeze(1).broadcast_to([P, v.shape[1], HD]),
                                   ALU.mult).then_inc(tables_ready, 1)
            pool.wait_ge(tables_ready, 4)

            pool.wait_ge(tops_ready, 7)
            pool.partition_all_reduce(tops_all[:], tops[:], P, bass.bass_isa.ReduceOp.max).then_inc(tops_reduced, 1)

            def dequant(t):
                g, j = divmod(t, 4)
                v, vi = stage[:, g % 2, j, :], stage_i[:, g % 2, j, :]
                pool.wait_ge(wq_in[g % 2], 16 * (g // 2 + 1))
                pool.tensor_scalar(v, vi, -7.5, 1.0, ALU.add, ALU.mult).then_inc(deq_g1, 1)
                pool.wait_ge(deq_g1, t // 2 + 1)
                pool.wait_ge(scales_ready, 5)
                pool.tensor_tensor(v.rearrange("p (b c) -> p b c", c=QB), v.rearrange("p (b c) -> p b c", c=QB),
                                   scale_of(t), ALU.mult).then_inc(deq_g, 1)

            def attention(A, s):
                for c in range(BPB):
                    r = s - BASE[c]
                    n = 4 * A + c + 1
                    p = c % 2
                    if r == R_STATS:
                        pool.wait_ge(kv_in[c], 16 * A + 16)
                        kv = kvt[:, c, :]
                        after(pool, k_turned, n - 1)
                        pool.tensor_tensor(k_cos[:], kv, cwk[:], ALU.mult).then_inc(k_parts, 1)
                        pool.tensor_tensor(halves(k_sin[:], False), halves(kv, True), halves(swk[:], False),
                                           ALU.mult).then_inc(k_parts, 1)
                        pool.wait_ge(k_parts, 2 * n)
                        pool.tensor_tensor(k_sum[:], k_cos[:], k_sin[:], ALU.add).then_inc(k_summed, 1)
                        pool.wait_ge(norm_args, 2 * n)
                        pool.tensor_tensor(inv[:, p, :], arg[:, p, :], minus_half[:], ALU.pow).then_inc(norms, 1)
                        pool.wait_ge(norms, n)
                        pool.wait_ge(k_summed, n)
                        pool.tensor_tensor(k[:], k_sum[:], inv[:, p, 1:2].broadcast_to([P, CK]), ALU.mult).then_inc(k_ready, 1)
                    if r == R_CENTRE:
                        pool.wait_ge(x_centred, n)
                        pool.tensor_tensor(t_cos[:], xc[:], cw[:], ALU.mult).then_inc(q_cos, 1)
                    if r in (R_SCORES[0] + 1, R_SCORES[1] + 1):
                        for m in ((0, 1) if r == R_SCORES[0] + 1 else (2, 3)):
                            pool.wait_ge(inv_sums, 2 * (n - 1) + m // 2 + 1)
                            pool.tensor_tensor(pr[:, m], pr[:, m],
                                               rinv[:, p, 4 * m:4 * m + 4].unsqueeze(2).broadcast_to([P, NG, P]),
                                               ALU.mult).then_inc(probs, 1)
                    if r == R_PROJ:
                        pool.wait_ge(arg2_ready, n)
                        pool.tensor_tensor(inv2[:, p:p + 1], arg2[:, p:p + 1], minus_half[:, 0:1],
                                           ALU.pow).then_inc(norm2, 1)

            def residual(F, c):
                pool.wait_ge(x1_ready, 4 * F + c + 1)
                pool.wait_ge(y_free[c], 16 * F + 16)
                pool.tensor_tensor(y[:, c, :], x1[:, c, :], bd_bc[:], ALU.add).then_inc(y_base, 1)

            for s in range(SLOTS):
                if s == 0:
                    dequant(1)
                    dequant(3)
                if s + 4 < 32 and (s + 4) % 2:
                    dequant(s + 4)
                attention(0, s)
            with pool.Fori(0, NBLK - 1) as i:
                for s in range(SLOTS):
                    if s < BPB:
                        residual(i, s)
                    attention(i + 1, s)
            for c in range(BPB):
                residual(NBLK - 1, c)

        @block.scalar
        def _(act):
            for src, dst in ((ident_d, ident), (causal, mask), (cos_t, cos_s), (sin_t, sin_s)):
                act.dma_start(dst[:], src).then_inc(consts_in, 16)
            act.dma_start(s_up[:], wus.rearrange("(c p) b -> p c b", p=P)).then_inc(scales_in, 16)
            act.dma_start(s_dn[:], wds.rearrange("(c p) b -> p c b", p=P)).then_inc(scales_in, 16)
            act.dma_start(b_up[:], bu.rearrange("(c p) -> p c", p=P), allow_slow_non_contiguous=True).then_inc(scales_in, 16)
            act.dma_start(a_nat[:, 0:KC * R].rearrange("p (c r) -> p c r", r=R),
                          wua.rearrange("(c p) r -> p c r", p=P)).then_inc(scales_in, 16)
            act.dma_start(a_nat[:, KC * R:].rearrange("p (c r) -> p c r", r=R),
                          wda.rearrange("(c p) r -> p c r", p=P)).then_inc(scales_in, 16)
            act.dma_start(b_up_lora, wub).then_inc(scales_in, 16)
            act.dma_start(b_dn_lora[:], wdb).then_inc(scales_in, 16)

            act.wait_ge(wout_in, 16)
            for j in range(KC):
                act.activation(wo_nat[:, j, :].rearrange("p (n g d) -> p n g d", g=NG, d=HD),
                               pr[:, j].rearrange("p a t -> p (a t)").rearrange("p (g n d) -> p n g d", g=NG, d=HD),
                               ACT.Copy).then_inc(wo_ordered, 1)

            act.wait_ge(a_turned, 1)
            act.activation(a_upT[:], ff[0][0:R, :], ACT.Copy).then_inc(a_copied, 1)
            for i in range(4):
                act.wait_ge(a_turned, i + 2)
                act.activation(a_dnT[:, 512 * i:512 * i + 512], ff[(i + 1) % 2][0:R, :], ACT.Copy).then_inc(a_copied, 1)
            for m in range(NN):
                act.wait_ge(wo_turned, m + 1)
                act.activation(wo_hi[:, m, :], ff[(m + 1) % 2][:], ACT.Copy).then_inc(wo_high, 1)

            def weights(s):
                act.wait_ge(w_turned, s + 1)
                dst = wu_hi[:, s % 4, 512 * (s // 4):512 * (s // 4) + 512] if s < 16 else wd_hi[:, s - 16, :]
                act.activation(dst, ff[s % 2][:], ACT.Copy).then_inc(w_high, 1)

            def attention(A, s):
                for c in range(BPB):
                    r = s - BASE[c]
                    n = 4 * A + c + 1
                    p = c % 2
                    if r == R_STATS:
                        act.wait_ge(kv_in[c], 16 * A + 16)
                        act.activation(sq_junk[:], kvt[:, c, :], ACT.Square, accum_out=ssq[:, p:p + 1]).then_inc(ctx_sq, 1)
                    if r == R_TURN:
                        act.wait_ge(q_turned, n)
                        act.activation(qT_hi[:].rearrange("p n t -> p (n t)"), tb[0][:], ACT.Copy).then_inc(q_high, 1)
                        act.wait_ge(k_turned, n)
                        act.wait_ge(diag_zero, 2)
                        for g in range(NG):
                            d = slice(HD * g, HD * g + HD)
                            last = act.activation(kD_hi[d, g, :], tb[1][d, 0:P], ACT.Copy)
                        last.then_inc(k_high, 1)
                    if r in R_SCORES:
                        for m in ((0, 1) if r == R_SCORES[0] else (2, 3)):
                            act.wait_ge(row_max, 4 * (n - 1) + m + 1)
                            for g in range(NG):
                                j = 4 * m + g
                                last = act.activation(pr[:, m, g, :], pr[:, m, g, :], ACT.Exp,
                                                      bias=nmax[:, p, j:j + 1], scale=-1.0,
                                                      accum_out=rsum[:, p, j:j + 1])
                            last.then_inc(exps, 1)
                    if r in R_PT:
                        for m in ((0, 1) if r == R_PT[0] else (2, 3)):
                            act.wait_ge(probs_turned, 4 * (n - 1) + m + 1)
                            act.activation(prT[:, :, m, :], tb[m % 2][:].rearrange("p (g t) -> p g t", g=NG),
                                           ACT.Copy).then_inc(probsT, 1)
                    if r == R_PV:
                        act.wait_ge(heads_out, n)
                        act.activation(oT_hi[:].rearrange("p n t -> p (n t)"), pvb[:], ACT.Copy).then_inc(o_high, 1)
                    if s == TURN2[c]:
                        act.wait_ge(xn2_turned, n)
                        act.activation(xnT_hi[:, :, P * c:P * c + P], prb[:].rearrange("p (k t) -> p k t", k=KC),
                                       ACT.Copy, scale=XN_SCALE).then_inc(xn_high, 1)

            def hidden(F, h):
                act.wait_ge(up_done, 16 * F + h + 1)
                if h >= 2:
                    act.wait_ge(x2_low, 16 * F + h - 1)
                act.activation(relu[:, h % 2, :], ff[h % 2][:], ACT.Relu, bias=b_up[:, h:h + 1],
                               scale=su[:]).then_inc(relu_done, 1)
                act.wait_ge(relu_done, 16 * F + h + 1)
                act.activation(x2_hi[:, h, :], relu[:, h % 2, :], ACT.Copy).then_inc(x2_high, 1)

            def store(F, t):
                act.wait_ge(down_read, 4 * F + 4 + t + 1)
                act.dma_start(out_v[4 * F + t], y[:, t, :]).then_inc(y_free[t], 16)

            def feed_forward(F, s):
                if 1 <= s <= 16:
                    hidden(F, s - 1)
                if s in (20, 24, 28):
                    store(F, (s - 20) // 4)

            for s in range(SLOTS):
                attention(0, s)
                weights(s)
            act.wait_ge(scales_ready, 5)
            with act.Fori(0, NBLK - 1) as i:
                for s in range(SLOTS):
                    attention(i + 1, s)
                    feed_forward(i, s)
                store(i, 3)
            for s in range(SLOTS):
                feed_forward(NBLK - 1, s)
            store(NBLK - 1, 3)
            for t in range(BPB):
                act.wait_ge(y_free[t], 16 * NBLK + 16)

        @block.tensor
        def _(pe):
            def turn(dst, src, **kw):
                return pe.matmul(dst, src, ident[0:src.shape[0], 0:src.shape[0]], is_transpose=True, **kw)

            pe.wait_ge(consts_in, 16 * 4)
            pe.wait_ge(scales_in, 16 * 7)
            for i in range(5):
                if i >= 2:
                    pe.wait_ge(a_copied, i - 1)
                for j in range(4):
                    b = 4 * i + j
                    last = turn(ff[i % 2][0:R, P * j:P * j + P], a_nat[:, R * b:R * b + R], start=True, stop=True)
                last.then_inc(a_turned, 1)
            pe.wait_ge(wo_ordered, KC)
            for m in range(NN):
                if m < 2:
                    pe.wait_ge(a_copied, m + 4)
                else:
                    pe.wait_ge(wo_low, m - 1)
                for j in range(KC):
                    last = turn(ff[(m + 1) % 2][:, P * j:P * j + P], wo_nat[:, j, P * m:P * m + P], start=True, stop=True)
                last.then_inc(wo_turned, 1)

            def weights(s):
                if s < 2:
                    pe.wait_ge(wo_low, NN)
                elif s < 30:
                    pe.wait_ge(w_low, s - 1)
                else:
                    pe.wait_ge(down_read, s - 29)
                g, j = divmod(s, 4)
                if s == 0:
                    pe.wait_ge(scales_ready, 5)
                if s < 16:
                    a, b = a_upT[:, P * j:P * j + P], b_up_lora[:, 512 * g:512 * g + 512]
                else:
                    a, b = a_dnT[:, P * (s - 16):P * (s - 16) + P], b_dn_lora[:]
                lora = pe.matmul(ff[s % 2][:], a, b, start=True, stop=False, skip_group_check=True)
                if s < BPB:
                    lora.then_inc(y_free[s], 16)
                if j == 0:
                    pe.wait_ge(deq_v, 2 * g + 2)
                    pe.wait_ge(deq_g, 2 * g + 2)
                for t in range(4):
                    last = turn(ff[s % 2][:, P * t:P * t + P], stage[:, g % 2, t, P * j:P * j + P],
                                start=False, stop=(t == 3), skip_group_check=True)
                last.then_inc(w_turned, 1)

            def attention(A, s):
                for c in range(BPB):
                    r = s - BASE[c]
                    n = 4 * A + c + 1
                    if r == R_TURN:
                        after(pe, probsT, 4 * (n - 1))
                        pe.wait_ge(q_ready, n)
                        for m in range(NN):
                            last = turn(tb[0][:, P * m:P * m + P], q[:, P * m:P * m + P], start=True, stop=True)
                        last.then_inc(q_turned, 1)
                        pe.wait_ge(k_ready, n)
                        turn(tb[1][:, 0:P], k[:], start=True, stop=True).then_inc(k_turned, 1)
                    if r in R_SCORES:
                        for m in ((0, 1) if r == R_SCORES[0] else (2, 3)):
                            if m == 0:
                                pe.wait_ge(q_low, n)
                                pe.wait_ge(k_low, n)
                            after(pe, masked, 4 * (n - 1) + m - 1)
                            terms = ((qT_hi, kD_hi), (qT_lo, kD_hi), (qT_hi, kD_lo))
                            for i, (a, b) in enumerate(terms):
                                last = pe.matmul(sbk[m % 2][:], a[:, m, :], b[:].rearrange("p g t -> p (g t)"),
                                                 start=(i == 0), stop=(i == 2))
                            last.then_inc(scores, 1)
                    if r in R_PT:
                        for m in ((0, 1) if r == R_PT[0] else (2, 3)):
                            pe.wait_ge(probs, 4 * (n - 1) + m + 1)
                            if m == 0:
                                pe.wait_ge(q_low, n)
                            elif m == 1:
                                pe.wait_ge(k_low, n)
                            else:
                                pe.wait_ge(probsT, 4 * (n - 1) + m - 1)
                            for g in range(NG):
                                last = turn(tb[m % 2][:, P * g:P * g + P], pr[:, m, g, :], start=True, stop=True)
                            last.then_inc(probs_turned, 1)
                    if r == R_PV:
                        pe.wait_ge(probsT, 4 * n)
                        after(pe, o_low, n - 1)
                        for g in range(NG):
                            d = slice(HD * g, HD * g + HD)
                            last = pe.matmul(pvb[d, :], kvt[:, c, d], prT[:, g].rearrange("p n t -> p (n t)"),
                                             start=True, stop=True)
                        last.then_inc(heads_out, 1)
                    if r == R_PROJ:
                        pe.wait_ge(o_low, n)
                        after(pe, x1_ready, n - 1)
                        after(pe, xn_low, 4 * A + (0, 0, 2, 3)[c])
                        if isinstance(A, int) and c == 0:
                            pe.wait_ge(wo_low, NN)
                        terms = ((oT_hi, wo_hi), (oT_lo, wo_hi), (oT_hi, wo_lo))
                        for i, (a, b) in enumerate(terms):
                            for m in range(NN):
                                last = pe.matmul(prb[:], a[:, m, :], b[:, m, :],
                                                 start=(i == 0 and m == 0), stop=(i == 2 and m == NN - 1))
                        last.then_inc(projected, 1)
                    if s == TURN2[c]:
                        pe.wait_ge(xn2_ready, n)
                        pe.wait_ge(x1_ready, 4 * A + (2, 2, 3, 4)[c])
                        after(pe, xn_low, n - 1)
                        for m in range(KC):
                            last = turn(prb[:, P * m:P * m + P], xn2[:, c % 2, P * m:P * m + P], start=True, stop=True)
                        last.then_inc(xn2_turned, 1)

            def feed_forward(F, s):
                if s < HC:
                    if s == 0:
                        pe.wait_ge(xn_low, 4 * F + 4)
                    if s < 2:
                        pe.wait_ge(down_read, 4 * F + 3 + s)
                    else:
                        pe.wait_ge(relu_done, 16 * F + s - 1)
                    terms = ((wu_hi, xnT_hi), (wu_hi, xnT_lo), (wu_lo, xnT_hi))
                    for m in range(KC):
                        for i, (a, b) in enumerate(terms):
                            last = pe.matmul(ff[s % 2][:], a[:, m, P * s:P * s + P], b[:, m, :],
                                             start=(m == 0 and i == 0), stop=(m == KC - 1 and i == 2))
                    last.then_inc(up_done, 1)
                else:
                    t, part = divmod(s - HC, 4)
                    if part == 0:
                        if t < 2:
                            pe.wait_ge(relu_done, 16 * F + 15 + t)
                        else:
                            pe.wait_ge(down_read, 4 * F + 4 + t - 1)
                    terms = ((x2_hi, wd_hi), (x2_lo, wd_hi), (x2_hi, wd_lo))
                    for h in range(4 * part, 4 * part + 4):
                        if t == 0:
                            pe.wait_ge(x2_low, 16 * F + h + 1)
                        for i, (a, b) in enumerate(terms):
                            last = pe.matmul(ff[t % 2][:], a[:, h, P * t:P * t + P], b[:, h, :],
                                             start=(h == 0 and i == 0), stop=(h == HC - 1 and i == 2))
                    if part == 3:
                        last.then_inc(down_done, 1)

            for s in range(SLOTS):
                attention(0, s)
                weights(s)
            pe.wait_ge(w_low, 28)
            pe.wait_ge(down_read, 4)
            with pe.Fori(0, NBLK - 1) as i:
                for s in range(SLOTS):
                    attention(i + 1, s)
                    feed_forward(i, s)
            for s in range(SLOTS):
                feed_forward(NBLK - 1, s)

        @block.vector
        def _(dve):
            dve.memset(tops[:], 0.0).then_inc(tops_zero, 1)
            dve.wait_ge(tops_zero, 1)
            dve.wait_ge(scales_in, 16 * 7)
            for j, v in enumerate((s_up[:].rearrange("p a b -> p (a b)"), s_dn[:].rearrange("p a b -> p (a b)"),
                                   a_nat[:, 0:KC * R], a_nat[:, KC * R:], b_up_lora, b_dn_lora[:], b_up[:])):
                dve.tensor_reduce(tops[0:v.shape[0], j:j + 1], v, AXX, ALU.max,
                                  apply_absolute_value=True).then_inc(tops_ready, 1)
            dve.wait_ge(tops_reduced, 1)
            step = [0]

            def link(ins):
                step[0] += 1
                ins.then_inc(scale_steps, 1)
                dve.wait_ge(scale_steps, step[0])

            lora, deq, wtop, wpow, ytop = (tmp[:, 2 * i:2 * i + 2] for i in range(5))
            link(dve.tensor_tensor(lora, tops_all[:, 2:4], tops_all[:, 4:6], ALU.mult))
            link(dve.tensor_scalar(deq, tops_all[:, 0:2], 7.5, 1e-30, ALU.mult, ALU.add))
            link(dve.scalar_tensor_tensor(wtop, lora, float(R), deq, ALU.mult, ALU.add))
            link(dve.scalar_tensor_tensor(ytop[:, 0:1], wtop[:, 0:1], float(C), tops_all[:, 6:7], ALU.mult, ALU.add))
            link(dve.tensor_scalar(wpow.bitcast(I32), wtop.bitcast(I32), 0x7F800000, None, ALU.bitwise_and))
            link(dve.tensor_scalar(ytop[:, 1:2].bitcast(I32), ytop[:, 0:1].bitcast(I32), 0x7F800000, None, ALU.bitwise_and))
            link(dve.reciprocal(kap[:, 0:2], wpow))
            link(dve.reciprocal(kap[:, 2:3], ytop[:, 1:2]))
            link(dve.tensor_scalar(kap[:, 0:2], kap[:, 0:2], W_TOP, None, ALU.mult))
            link(dve.tensor_scalar(kap[:, 2:3], kap[:, 2:3], X2_TOP, None, ALU.mult))
            link(dve.tensor_scalar(su[:], wpow[:, 0:1], kap[:, 2:3], 1.0 / (W_TOP * XN_SCALE), ALU.mult, ALU.mult))
            link(dve.tensor_scalar(sd[:], wpow[:, 1:2], ytop[:, 1:2], 1.0 / (W_TOP * X2_TOP), ALU.mult, ALU.mult))
            for v, kx in ((s_up[:], kap[:, 0:1]), (s_dn[:], kap[:, 1:2]), (b_up_lora, kap[0:R, 0:1]),
                          (b_dn_lora[:], kap[0:R, 1:2]), (b_up[:], kap[:, 2:3])):
                dve.tensor_scalar(v, v, kx, None, ALU.mult).then_inc(scales_ready, 1)
            dve.wait_ge(scales_ready, 5)
            for m in range(NN):
                dve.wait_ge(wo_high, m + 1)
                dve.tensor_tensor(wo_lo[:, m, :], ff[(m + 1) % 2][:], wo_hi[:, m, :].bitcast(F32),
                                  ALU.subtract).then_inc(wo_low, 1)

            def dequant(t):
                g, j = divmod(t, 4)
                dve.wait_ge(wq_in[g % 2], 16 * (g // 2 + 1))
                dve.scalar_tensor_tensor(stage[:, g % 2, j, :].rearrange("p (b c) -> p b c", c=QB),
                                         stage_i[:, g % 2, j, :].rearrange("p (b c) -> p b c", c=QB), -7.5,
                                         scale_of(t), ALU.add, ALU.mult).then_inc(deq_v, 1)

            def weights(s):
                dve.wait_ge(w_high, s + 1)
                cols = slice(512 * (s // 4), 512 * (s // 4) + 512)
                hi, lo = ((wu_hi[:, s % 4, cols], wu_lo[:, s % 4, cols]) if s < 16 else
                          (wd_hi[:, s - 16, :], wd_lo[:, s - 16, :]))
                dve.tensor_tensor(lo, ff[s % 2][:], hi, ALU.subtract).then_inc(w_low if s < 28 else down_read, 1)

            def attention(A, s):
                for c in range(BPB):
                    r = s - BASE[c]
                    n = 4 * A + c + 1
                    p = c % 2
                    if r == R_STATS:
                        dve.wait_ge(x_in[c], 16 * A + 16)
                        dve.bn_stats(stats[:, p, :], xt[:, c, :]).then_inc(x_stats, 1)
                        dve.wait_ge(ctx_sq, n)
                        dve.wait_ge(x_stats, n)
                        dve.tensor_scalar(arg[:, p, 1:2], ssq[:, p:p + 1], 1.0 / CK, EPS,
                                          ALU.mult, ALU.add).then_inc(norm_args, 1)
                        dve.bn_aggr(mv[:, p, :], stats[:, p, :]).then_inc(x_moments, 1)
                        dve.wait_ge(x_moments, n)
                        dve.tensor_scalar(arg[:, p, 0:1], mv[:, p, 1:2], 1.0 + EPS, EPS * EPS,
                                          ALU.mult, ALU.add).then_inc(norm_args, 1)
                    if r == R_CENTRE:
                        dve.wait_ge(norms, n)
                        after(dve, q_cos, n - 1)
                        dve.tensor_scalar(xc[:], xt[:, c, :], mv[:, p, 0:1], inv[:, p, 0:1],
                                          ALU.subtract, ALU.mult).then_inc(x_centred, 1)
                        dve.wait_ge(x_centred, n)
                        dve.tensor_tensor(halves(t_sin[:], False), halves(xc[:], True), halves(sw[:], False),
                                          ALU.mult).then_inc(q_sin, 1)
                    if r == R_ROPE:
                        dve.wait_ge(q_cos, n)
                        dve.wait_ge(q_sin, n)
                        after(dve, q_turned, n - 1)
                        dve.tensor_tensor(q[:].rearrange("p (n g d) -> p g n d", g=NG, d=HD),
                                          t_cos[:].rearrange("p (g n d) -> p g n d", g=NG, d=HD),
                                          t_sin[:].rearrange("p (g n d) -> p g n d", g=NG, d=HD),
                                          ALU.add).then_inc(q_ready, 1)
                    if r == R_TURN:
                        dve.wait_ge(q_high, n)
                        dve.tensor_tensor(qT_lo[:].rearrange("p n t -> p (n t)"), tb[0][:],
                                          qT_hi[:].rearrange("p n t -> p (n t)").bitcast(F32),
                                          ALU.subtract).then_inc(q_low, 1)
                        dve.wait_ge(k_high, n)
                        dve.wait_ge(diag_zero, 2)
                        for g in range(NG):
                            d = slice(HD * g, HD * g + HD)
                            last = dve.tensor_tensor(kD_lo[d, g, :], tb[1][d, 0:P], kD_hi[d, g, :].bitcast(F32),
                                                     ALU.subtract)
                        last.then_inc(k_low, 1)
                    if r in R_SCORES:
                        ms = (0, 1) if r == R_SCORES[0] else (2, 3)
                        for m in ms:
                            dve.wait_ge(scores, 4 * (n - 1) + m + 1)
                            dve.scalar_tensor_tensor(pr[:, m], sbk[m % 2][:].rearrange("p (g t) -> p g t", g=NG), -SC,
                                                     mask[:].unsqueeze(1).broadcast_to([P, NG, P]),
                                                     ALU.mult, ALU.add).then_inc(masked, 1)
                        for m in ms:
                            dve.wait_ge(masked, 4 * (n - 1) + m + 1)
                            dve.tensor_reduce(nmax[:, p, 4 * m:4 * m + 4], pr[:, m], AXX, ALU.min).then_inc(row_max, 1)
                    if r in (R_SCORES[0] + 1, R_SCORES[1] + 1):
                        m = 0 if r == R_SCORES[0] + 1 else 2
                        dve.wait_ge(exps, 4 * (n - 1) + m + 2)
                        dve.reciprocal(rinv[:, p, 4 * m:4 * m + 8], rsum[:, p, 4 * m:4 * m + 8]).then_inc(inv_sums, 1)
                    if r == R_PV:
                        dve.wait_ge(o_high, n)
                        dve.tensor_tensor(oT_lo[:].rearrange("p n t -> p (n t)"), pvb[:],
                                          oT_hi[:].rearrange("p n t -> p (n t)").bitcast(F32),
                                          ALU.subtract).then_inc(o_low, 1)
                    if r == R_PROJ:
                        dve.wait_ge(projected, n)
                        after(dve, y_base, n - 4)
                        dve.tensor_tensor(x1[:, c, :], prb[:], xt[:, c, :], ALU.add).then_inc(x1_ready, 1)
                        dve.wait_ge(x1_ready, n)
                        dve.bn_stats(stats2[:, p, :], x1[:, c, :]).then_inc(x1_stats, 1)
                        dve.wait_ge(x1_stats, n)
                        dve.memset(spare[:], 0.0)
                        dve.bn_aggr(mv2[:, p, :], stats2[:, p, :]).then_inc(x1_moments, 1)
                        dve.wait_ge(x1_moments, n)
                        dve.tensor_scalar(arg2[:, p:p + 1], mv2[:, p, 1:2], EPS, None, ALU.add).then_inc(arg2_ready, 1)
                    if r == R_NORM2:
                        dve.wait_ge(norm2, n)
                        after(dve, xn2_turned, n - 2)
                        dve.tensor_scalar(xn2[:, p, :], x1[:, c, :], mv2[:, p, 0:1], inv2[:, p:p + 1],
                                          ALU.subtract, ALU.mult).then_inc(xn2_ready, 1)
                    if s == TURN2[c]:
                        dve.wait_ge(xn_high, n)
                        dve.scalar_tensor_tensor(xnT_lo[:, :, P * c:P * c + P], prb[:].rearrange("p (k t) -> p k t", k=KC),
                                                 XN_SCALE, xnT_hi[:, :, P * c:P * c + P],
                                                 ALU.mult, ALU.subtract).then_inc(xn_low, 1)

            def result(F, t):
                dve.wait_ge(down_done, 4 * F + t + 1)
                dve.wait_ge(y_base, 4 * F + t + 1)
                dve.scalar_tensor_tensor(y[:, t, :], ff[t % 2][:], sd[:], y[:, t, :],
                                         ALU.mult, ALU.add).then_inc(down_read, 1)

            def feed_forward(F, s):
                if 1 <= s <= 16:
                    h = s - 1
                    dve.wait_ge(x2_high, 16 * F + h + 1)
                    dve.tensor_tensor(x2_lo[:, h, :], relu[:, h % 2, :], x2_hi[:, h, :], ALU.subtract).then_inc(x2_low, 1)
                if s in (20, 24, 28):
                    result(F, (s - 20) // 4)

            for s in range(SLOTS):
                if s == 0:
                    dequant(0)
                    dequant(2)
                if s + 4 < 32 and (s + 4) % 2 == 0:
                    dequant(s + 4)
                attention(0, s)
                weights(s)
            with dve.Fori(0, NBLK - 1) as i:
                for s in range(SLOTS):
                    attention(i + 1, s)
                    feed_forward(i, s)
                result(i, 3)
            for s in range(SLOTS):
                feed_forward(NBLK - 1, s)
            result(NBLK - 1, 3)


_INS = ["x", "ctx_512", "L0_xattn_q_norm_w", "L0_xattn_k_norm_w", "L0_xattn_w_out",
        "L0_ffn_w_up_q", "L0_ffn_w_up_scale", "L0_ffn_b_up", "L0_ffn_w_up_lora_a", "L0_ffn_w_up_lora_b",
        "L0_ffn_w_down_q", "L0_ffn_w_down_scale", "L0_ffn_b_down", "L0_ffn_w_down_lora_a", "L0_ffn_w_down_lora_b"]


def shape_tables(T=128, HD=32, theta=10000.0):
    f = np.float32
    inv_freq = f(1.0) / np.power(f(theta), np.arange(0, HD, 2, dtype=f) / f(HD)).astype(f)
    freqs = np.outer(np.arange(T, dtype=f), inv_freq).astype(f)
    emb = np.concatenate([freqs, freqs], -1)
    sin = np.sin(emb).astype(f)
    sin[:, :HD // 2] *= f(-1.0)
    causal = np.where(np.tril(np.ones((T, T), bool)), f(0), f(BIG)).astype(f)
    return {"cos_t": np.cos(emb).astype(f), "sin_t": sin, "causal": causal, "ident": np.eye(T, dtype=f)}


def kernel(**inputs):
    import concourse.bacc as _bacc
    from concourse import mybir as _mybir
    from concourse.bass_utils import run_bass_kernel_spmd as _run

    nc = _bacc.Bacc("TRN2", target_bir_lowering=False, num_devices=1)
    arrays, args = {}, []
    for name, a in [(n, inputs[n]) for n in _INS] + list(shape_tables().items()):
        a = np.ascontiguousarray(a)
        arrays[f"in_{name}"] = a
        args.append(nc.dram_tensor(f"in_{name}", a.shape, _mybir.dt.from_np(a.dtype), kind="ExternalInput").ap())
    args.append(nc.dram_tensor("out_0", tuple(inputs["x"].shape), _mybir.dt.float32, kind="ExternalOutput").ap())
    build(nc, *args)
    r = _run(nc, [arrays], core_ids=[0])
    return r.results[0]["out_0"]
```

```python
from contextlib import ExitStack

import concourse.bass as bass
import numpy as np
from concourse import mybir

F32 = mybir.dt.float32
F32R = mybir.dt.float32r
F16 = mybir.dt.float16
I32 = mybir.dt.int32
ALU = mybir.AluOpType
ACT = mybir.ActivationFunctionType
AXX = mybir.AxisListType.X

P = 128
EPS = 1e-5
SCALE_STEPS = 17
XN_SCALE = 1024.0
W_TOP, A_TOP, X2_TOP = 2.0 ** 13, 2.0 ** 10, 2.0 ** 14
BIG = 1e30

BPB = 4
SLOTS = 32
BASE = (0, 5, 11, 16)
R_STATS, R_CENTRE, R_ROPE = 0, 1, 2
R_KTURN, R_QTURN, R_QSPLIT = 2, 2, 3
R_SCORES = (3, 4, 5, 6)
R_MASK = (4, 5, 6, 7)
R_EXP = (5, 6, 7, 8)
R_PROBS = (6, 7, 8, 9)
R_PT = (7, 8, 9, 10)
R_PV, R_PROJ, R_X1, R_NORM2 = 11, 12, 13, 14
TURN2 = (20, 22, 26, 31)
WOUT_AT = 3
DEQ_LEAD = 4
LAG = 2


def build(nc, x, ctx, qw, kw, wo, wuq, wus, bu, wua, wub, wdq, wds, bd, wda, wdb,
          tabs_d, out):
    B, T, C = x.shape
    CK = ctx.shape[2]
    HD, NG = 32, 4
    NN = C // HD // NG
    H = wuq.shape[0]
    R = wua.shape[1]
    KC, HC = C // P, H // P
    NBLK = B // BPB
    QB = 64
    SC = float(np.float32(1.0) / np.sqrt(np.float32(HD)))
    assert T == P and CK == P and NBLK == 4 and HC == 16 and KC == 4 and NN == 4

    with ExitStack() as es:
        def sb(name, shape, dt=F32):
            return es.enter_context(nc.sbuf_tensor(name, shape, dt))

        def sem(name):
            return es.enter_context(nc.semaphore(name))

        wu_hi, wu_lo = sb("wu_hi", [P, KC, H], F16), sb("wu_lo", [P, KC, H], F16)
        wd_hi, wd_lo = sb("wd_hi", [P, HC, C], F16), sb("wd_lo", [P, HC, C], F16)
        wo_hi, wo_lo = sb("wo_hi", [P, NN, C], F32R), sb("wo_lo", [P, NN, C], F32R)
        xnT_hi, xnT_lo = sb("xnT_hi", [P, KC, BPB * P], F16), sb("xnT_lo", [P, KC, BPB * P], F16)
        big = sb("big", [P, 8192])
        x2_hi = big[:, 0:4096].bitcast(F16).rearrange("p (h t) -> p h t", h=HC)
        x2_lo = big[:, 4096:8192].bitcast(F16).rearrange("p (h t) -> p h t", h=HC)
        stage = big[:].rearrange("p (b j c) -> p b j c", b=4, j=4)
        stage_i = big[:].bitcast(I32).rearrange("p (b j c) -> p b j c", b=4, j=4)
        low_area = wd_lo[:].rearrange("p h c -> p (h c)").bitcast(F32)
        high_area = wd_hi[:].rearrange("p h c -> p (h c)").bitcast(F32)
        wo_raw = low_area[:, 0:2048].rearrange("p (j c) -> p j c", c=C)
        a_nat = low_area[:, 3072:3072 + (KC + HC) * R]
        a_parts = (low_area[:, 3392:3392 + (KC + HC) * R * 3 // 2].bitcast(F16)
                   .rearrange("p (c k r) -> p c k r", k=3, r=R))
        b_up_flat = high_area[:, 2048:2048 + R * H // P]
        b_dn_flat = high_area[:, 2304:2304 + R * C // P]
        qw_bc, kw_bc = high_area[:, 2368:2368 + C], high_area[:, 2880:2880 + CK]
        relu = sb("relu", [P, 2, BPB * P])
        R3 = 3 * R
        b_up_in, b_dn_in = high_area[0:R3, 0:H], sb("b_dn_in", [R3, C])
        b_up3 = low_area[0:R3, 2048:3072].bitcast(F16)
        a_dn3 = relu[0:R3].rearrange("p a b -> p (a b)").bitcast(F16)
        a_up3, b_dn3 = sb("a_up3", [R3, C], F16), sb("b_dn3", [R3, C], F16)
        xt = sb("xt", [P, BPB, C])
        x1 = sb("x1", [P, BPB, C])
        y = sb("y", [P, BPB, C])
        kvt = sb("kvt", [P, BPB, CK])
        cw, sw = sb("cw", [P, C]), sb("sw", [P, C])
        cwk, swk = sb("cwk", [P, CK]), sb("swk", [P, CK])
        tabs = sb("tabs", [P, 2 * P + 2 * HD])
        ident, mask = tabs[:, 0:P], tabs[:, P:2 * P]
        cos_s, sin_s = tabs[:, 2 * P:2 * P + HD], tabs[:, 2 * P + HD:]
        bd_bc = sb("bd_bc", [P, C])
        xc = sb("xc", [P, C])
        t_cos, t_sin, q = sb("t_cos", [P, C]), sb("t_sin", [P, C]), sb("q", [P, C])
        k_cos, k_sin, k_sum, k = (sb(s, [P, CK]) for s in ("k_cos", "k_sin", "k_sum", "k"))
        sq_junk = sb("sq_junk", [P, CK])
        qT_hi, qT_lo = sb("qT_hi", [P, NN, P], F32R), sb("qT_lo", [P, NN, P], F32R)
        kD_hi, kD_lo = sb("kD_hi", [P, NG, P], F32R), sb("kD_lo", [P, NG, P], F32R)
        pr = sb("pr", [P, NN, NG, P])
        prT = sb("prT", [P, NG, NN, P])
        ident16 = sb("ident16", [P, P], F16)
        b_nat = sb("b_nat", [HC, P])
        oT_hi, oT_lo = sb("oT_hi", [P, NN, P], F32R), sb("oT_lo", [P, NN, P], F32R)
        xn2 = sb("xn2", [P, 2, C])
        stats, stats2 = sb("stats", [P, 2, 6]), sb("stats2", [P, 2, 6])
        spare = sb("spare", [P, 1])
        mv, mv2 = sb("mv", [P, 2, 2]), sb("mv2", [P, 2, 2])
        ssq = sb("ssq", [P, 2])
        arg, inv = sb("arg", [P, 2, 2]), sb("inv", [P, 2, 2])
        arg2, inv2 = sb("arg2", [P, 2]), sb("inv2", [P, 2])
        minus_half = sb("minus_half", [P, 2])
        nmax = sb("nmax", [P, 2, NN * NG])
        rsum, rinv = sb("rsum", [P, 2, NN * NG]), sb("rinv", [P, 2, NN * NG])
        s_up, s_dn = sb("s_up", [P, HC, C // QB]), sb("s_dn", [P, KC, H // QB])
        b_up = sb("b_up", [P, HC])
        tops, tops_all = sb("tops", [P, 8]), sb("tops_all", [P, 8])
        tmp = sb("tmp", [P, 16])
        kap = sb("kap", [P, 8])
        su, sd = sb("su", [P, 1]), sb("sd", [P, 1])

        def bank(name):
            return es.enter_context(nc.psum_tensor(name, [P, 512], F32))
        ff = [bank("ff0"), bank("ff1")]
        sbk = [bank("sb0"), bank("sb1")]
        tb = [bank("tb0"), bank("tb1")]
        pvb = bank("pvb")
        prb = bank("prb")

        norm_w_in = sem("norm_w_in")
        consts_in, scales_in, wout_in = sem("consts_in"), sem("scales_in"), sem("wout_in")
        b_in = sem("b_in")
        wq_in = [sem(f"wq_in{i}") for i in range(4)]
        down_bias_in, b_flat_in = sem("down_bias_in"), sem("b_flat_in")
        x_in = [sem(f"x_in{i}") for i in range(BPB)]
        kv_in = [sem(f"kv_in{i}") for i in range(BPB)]
        y_free = [sem(f"y_free{i}") for i in range(BPB)]
        tops_zero, tops_ready, tops_reduced = sem("tops_zero"), sem("tops_ready"), sem("tops_reduced")
        scale_steps, scales_ready = sem("scale_steps"), sem("scales_ready")
        tables_ready, pool_consts, diag_zero = sem("tables_ready"), sem("pool_consts"), sem("diag_zero")
        bias_scaled = sem("bias_scaled")
        a_high, a_low, b_high, b_low = sem("a_high"), sem("a_low"), sem("b_high"), sem("b_low")
        ident_cast, b_turned = sem("ident_cast"), sem("b_turned")
        a_turned, a_copied = sem("a_turned"), sem("a_copied")
        wo_ordered = sem("wo_ordered")
        wo_turned, wo_high, wo_low = sem("wo_turned"), sem("wo_high"), sem("wo_low")
        deq_v, deq_g, deq_g1 = sem("deq_v"), sem("deq_g"), sem("deq_g1")
        w_turned, w_high, w_low = sem("w_turned"), sem("w_high"), sem("w_low")
        x_stats, x_moments, ctx_sq = sem("x_stats"), sem("x_moments"), sem("ctx_sq")
        norm_args, norms = sem("norm_args"), sem("norms")
        x_centred, q_cos, q_sin, q_ready = sem("x_centred"), sem("q_cos"), sem("q_sin"), sem("q_ready")
        k_parts, k_summed, k_ready = sem("k_parts"), sem("k_summed"), sem("k_ready")
        q_turned, k_turned = sem("q_turned"), sem("k_turned")
        q_high, q_low, k_high, k_low = sem("q_high"), sem("q_low"), sem("k_high"), sem("k_low")
        scores, masked, row_max = sem("scores"), sem("masked"), sem("row_max")
        exps, inv_sums, probs = sem("exps"), sem("inv_sums"), sem("probs")
        probs_turned, probsT = sem("probs_turned"), sem("probsT")
        heads_out, o_high, o_low = sem("heads_out"), sem("o_high"), sem("o_low")
        projected, x1_ready = sem("projected"), sem("x1_ready")
        x1_stats, x1_moments, arg2_ready, norm2 = sem("x1_stats"), sem("x1_moments"), sem("arg2_ready"), sem("norm2")
        xn2_ready, xn2_turned, xn_high, xn_low = sem("xn2_ready"), sem("xn2_turned"), sem("xn_high"), sem("xn_low")
        up_done, relu_done, x2_high, x2_low = sem("up_done"), sem("relu_done"), sem("x2_high"), sem("x2_low")
        down_done, down_read, y_base = sem("down_done"), sem("down_read"), sem("y_base")

        wuq_v = wuq.rearrange("(g j p) c -> g p j c", p=P, j=4)
        wdq_v = wdq.rearrange("(j p) (g c) -> g p j c", p=P, c=512)
        out_v = out
        wo_nat = y

        def after(eng, s, value):
            if not isinstance(value, int) or value > 0:
                eng.wait_ge(s, value)

        def halves(v, swap):
            v = v.rearrange("p (h s d) -> p h s d", s=2, d=HD // 2)
            return v[:, :, ::-1, :] if swap else v

        def scale_of(t):
            g, j = divmod(t, 4)
            v = s_up[:, t, :] if g < 4 else s_dn[:, j, 8 * (g - 4):8 * (g - 4) + 8]
            return v.unsqueeze(2).broadcast_to([P, 8, QB])

        block = es.enter_context(nc.Block())

        def before(slots, s, itself=False):
            return sum(v < s or (itself and v == s) for v in slots)

        b_pieces = ((b_up3[:, 0:512], b_up_in[:, 0:512], 4), (b_up3[:, 512:], b_up_in[:, 512:], 4),
                    (b_dn3[:], b_dn_in[:], 5))

        def tiles_to_dequantise(s):
            t = s - LAG + DEQ_LEAD
            return range(DEQ_LEAD - LAG + 2) if s == 1 else range(t, t + 1) if 1 < s and t < SLOTS else ()

        PV_AT = tuple(v + R_PV for v in BASE)
        PROJ_AT = tuple(v + R_PROJ for v in BASE)

        @block.sync
        def _(sp):
            def load_batch(A, c):
                after(sp, x1_ready, 4 * A - 3 + c)
                sp.dma_start(xt[:, c, :], x[4 * A + c]).then_inc(x_in[c], 16)
                after(sp, heads_out, 4 * A - 3 + c)
                sp.dma_start(kvt[:, c, :], ctx[4 * A + c]).then_inc(kv_in[c], 16)

            def load_group(g):
                if g >= 4:
                    after(sp, w_turned, 4 * (g - 3))
                src = wuq_v[g] if g < 4 else wdq_v[g - 4]
                sp.dma_start(stage_i[:, g % 4], src).then_inc(wq_in[g % 4], 16)

            sp.dma_start(s_up[:], wus.rearrange("(c p) b -> p c b", p=P)).then_inc(scales_in, 16)
            sp.dma_start(s_dn[:], wds.rearrange("(c p) b -> p c b", p=P)).then_inc(scales_in, 16)
            load_batch(0, 0)
            for src, dst in ((kw, kw_bc), (qw, qw_bc)):
                n = src.shape[0]
                sp.dma_start(dst, src.rearrange("(a n) -> a n", a=1).broadcast_to([P, n])).then_inc(norm_w_in, 16)
            load_group(0)
            for i in range(3):
                sp.dma_start(b_up_in[R * i:R * i + R], wub).then_inc(b_in, 16)
                sp.dma_start(b_dn_in[R * i:R * i + R], wdb).then_inc(b_in, 16)
            sp.dma_start(wo_raw, wo.rearrange("(j p) c -> p j c", p=P)).then_inc(wout_in, 16)
            load_batch(0, 1)
            load_group(1)
            load_batch(0, 2)
            load_group(2)
            load_group(3)
            load_batch(0, 3)
            sp.dma_start(bd_bc[:], bd.rearrange("(a n) -> a n", a=1).broadcast_to([P, C])).then_inc(down_bias_in, 16)
            for g in range(4, 8):
                load_group(g)
            with sp.Fori(0, NBLK - 1) as i:
                for c in range(BPB):
                    load_batch(i + 1, c)

        @block.gpsimd
        def _(pool):
            pool.dma_start(b_up_flat, wub.rearrange("r (a c) -> (r a) c", a=P // R)).then_inc(b_flat_in, 16)
            pool.dma_start(b_dn_flat, wdb.rearrange("r (a c) -> (r a) c", a=P // R)).then_inc(b_flat_in, 16)
            pool.memset(minus_half[:], -0.5).then_inc(pool_consts, 1)
            for t in (kD_hi, kD_lo):
                pool.memset(t[:].bitcast(F32), 0.0).then_inc(diag_zero, 1)

            def rotary_tables(*tables):
                for dst, w, tab, swap in tables:
                    n = w.shape[1] // HD
                    pool.tensor_tensor(halves(dst[:], False), halves(w, swap),
                                       tab.rearrange("p (s d) -> p s d", s=2).unsqueeze(1).broadcast_to([P, n, 2, HD // 2]),
                                       ALU.mult).then_inc(tables_ready, 1)

            def dequant(t):
                g, j = divmod(t, 4)
                v, vi = stage[:, g % 4, j, :], stage_i[:, g % 4, j, :]
                pool.wait_ge(wq_in[g % 4], 16 * (g // 4 + 1))
                pool.tensor_scalar(v, vi, -7.5, 1.0, ALU.add, ALU.mult).then_inc(deq_g1, 1)
                pool.wait_ge(deq_g1, t // 2 + 1)
                pool.wait_ge(scales_ready, 2)
                pool.tensor_tensor(v.rearrange("p (b c) -> p b c", c=QB), v.rearrange("p (b c) -> p b c", c=QB),
                                   scale_of(t), ALU.mult).then_inc(deq_g, 1)

            def probabilities(A, s):
                for c in range(BPB):
                    r = s - BASE[c]
                    n = 4 * A + c + 1
                    p = c % 2
                    if r in R_PROBS:
                        m = r - R_PROBS[0]
                        pool.wait_ge(inv_sums, 4 * (n - 1) + m + 1)
                        pool.tensor_tensor(pr[:, m], pr[:, m],
                                           rinv[:, p, 4 * m:4 * m + 4].unsqueeze(2).broadcast_to([P, NG, P]),
                                           ALU.mult).then_inc(probs, 1)

            def attention(A, s):
                for c in range(BPB):
                    r = s - BASE[c]
                    n = 4 * A + c + 1
                    p = c % 2
                    if r == R_STATS:
                        pool.wait_ge(kv_in[c], 16 * A + 16)
                        kv = kvt[:, c, :]
                        after(pool, k_turned, n - 1)
                        pool.tensor_tensor(k_cos[:], kv, cwk[:], ALU.mult).then_inc(k_parts, 1)
                        pool.tensor_tensor(halves(k_sin[:], False), halves(kv, True), halves(swk[:], False),
                                           ALU.mult).then_inc(k_parts, 1)
                        pool.wait_ge(k_parts, 2 * n)
                        pool.tensor_tensor(k_sum[:], k_cos[:], k_sin[:], ALU.add).then_inc(k_summed, 1)
                        pool.wait_ge(norm_args, 2 * n)
                        pool.tensor_tensor(inv[:, p, :], arg[:, p, :], minus_half[:], ALU.pow).then_inc(norms, 1)
                        pool.wait_ge(norms, n)
                        pool.wait_ge(k_summed, n)
                        pool.tensor_tensor(k[:], k_sum[:], inv[:, p, 1:2].broadcast_to([P, CK]), ALU.mult).then_inc(k_ready, 1)
                    if r == R_CENTRE:
                        pool.wait_ge(x_centred, n)
                        pool.tensor_tensor(t_cos[:], xc[:], cw[:], ALU.mult).then_inc(q_cos, 1)
                    if r == R_X1:
                        pool.wait_ge(arg2_ready, n)
                        pool.tensor_tensor(inv2[:, p:p + 1], arg2[:, p:p + 1], minus_half[:, 0:1],
                                           ALU.pow).then_inc(norm2, 1)

            def residual(F, c):
                pool.wait_ge(x1_ready, 4 * F + c + 1)
                pool.wait_ge(y_free[c], 16 * F + 16)
                pool.tensor_tensor(y[:, c, :], x1[:, c, :], bd_bc[:], ALU.add).then_inc(y_base, 1)

            pool.wait_ge(norm_w_in, 16 * 2)
            pool.wait_ge(consts_in, 16)
            rotary_tables((cwk, kw_bc, cos_s, False), (swk, kw_bc, sin_s, True))
            pool.wait_ge(tables_ready, 2)
            pool.wait_ge(tops_ready, 7)
            pool.partition_all_reduce(tops_all[:], tops[:], P, bass.bass_isa.ReduceOp.max).then_inc(tops_reduced, 1)
            attention(0, 0)
            rotary_tables((cw, qw_bc, cos_s, False), (sw, qw_bc, sin_s, True))
            pool.wait_ge(tables_ready, 4)
            for s in range(1, SLOTS + LAG):
                probabilities(0, s)
                for t in tiles_to_dequantise(s):
                    if t % 2:
                        dequant(t)
                attention(0, s)
            pool.wait_ge(down_bias_in, 16)
            with pool.Fori(0, NBLK - 1) as i:
                for s in range(SLOTS):
                    if s < BPB:
                        residual(i, s)
                    probabilities(i + 1, s)
                    attention(i + 1, s)
            for c in range(BPB):
                residual(NBLK - 1, c)

        @block.scalar
        def _(act):
            act.dma_start(tabs[:], tabs_d).then_inc(consts_in, 16)
            act.dma_start(a_nat[:, 0:KC * R].rearrange("p (c r) -> p c r", r=R),
                          wua.rearrange("(c p) r -> p c r", p=P)).then_inc(scales_in, 16)
            act.dma_start(a_nat[:, KC * R:].rearrange("p (c r) -> p c r", r=R),
                          wda.rearrange("(c p) r -> p c r", p=P)).then_inc(scales_in, 16)
            act.dma_start(b_nat[:], bu.rearrange("(c p) -> c p", p=P)).then_inc(scales_in, 16)

            def order_wout():
                act.wait_ge(wout_in, 16)
                for j in range(KC):
                    act.activation(wo_nat[:, j, :].rearrange("p (n g d) -> p n g d", g=NG, d=HD),
                                   wo_raw[:, j, :].rearrange("p (g n d) -> p n g d", g=NG, d=HD),
                                   ACT.Copy).then_inc(wo_ordered, 1)

            def wout_high(m):
                act.wait_ge(wo_turned, m + 1)
                act.activation(wo_hi[:, m, :], tb[m % 2][:], ACT.Copy).then_inc(wo_high, 1)

            def lora_high():
                act.wait_ge(scale_steps, SCALE_STEPS)
                for cols, chunks, kx in ((slice(0, KC * R), slice(0, KC), 2), (slice(KC * R, None), slice(KC, None), 3)):
                    src = a_nat[:, cols].rearrange("p (c r) -> p c r", r=R)
                    act.activation(a_parts[:, chunks, 0:3:2, :],
                                   src.unsqueeze(2).broadcast_to([P, src.shape[1], 2, R]),
                                   ACT.Identity, scale=kap[:, kx:kx + 1]).then_inc(a_high, 1)
                act.wait_ge(b_in, 16 * 6)
                for dst, src, kx in b_pieces:
                    act.activation(dst, src, ACT.Identity, scale=kap[0:R3, kx:kx + 1]).then_inc(b_high, 1)

            def lora_copy():
                for i, dst in enumerate((a_up3[:], a_dn3[:, 0:1024], a_dn3[:, 1024:2048])):
                    n = 1024 if i else 512
                    act.wait_ge(a_turned, i + 1)
                    act.activation(dst, ff[i % 2][0:R3, :].bitcast(F16)[:, 0:n], ACT.Copy).then_inc(a_copied, 1)

            def weights(s):
                act.wait_ge(w_turned, s + 1)
                dst = wu_hi[:, s % 4, 512 * (s // 4):512 * (s // 4) + 512] if s < 16 else wd_hi[:, s - 16, :]
                act.activation(dst, ff[s % 2][:], ACT.Copy).then_inc(w_high, 1)

            def exponentials(A, s):
                for c in range(BPB):
                    r = s - BASE[c]
                    n = 4 * A + c + 1
                    if r == R_QSPLIT:
                        act.wait_ge(q_turned, n)
                        act.activation(qT_hi[:].rearrange("p n t -> p (n t)"), prb[:], ACT.Copy).then_inc(q_high, 1)
                for c in range(BPB):
                    r = s - BASE[c]
                    n = 4 * A + c + 1
                    p = c % 2
                    if r in R_EXP:
                        m = r - R_EXP[0]
                        act.wait_ge(row_max, 4 * (n - 1) + m + 1)
                        for g in range(NG):
                            j = 4 * m + g
                            last = act.activation(pr[:, m, g, :], pr[:, m, g, :], ACT.Exp,
                                                  bias=nmax[:, p, j:j + 1], scale=-1.0,
                                                  accum_out=rsum[:, p, j:j + 1])
                        last.then_inc(exps, 1)

            def attention(A, s):
                for c in range(BPB):
                    r = s - BASE[c]
                    n = 4 * A + c + 1
                    p = c % 2
                    if r == R_STATS:
                        act.wait_ge(kv_in[c], 16 * A + 16)
                        act.activation(sq_junk[:], kvt[:, c, :], ACT.Square, accum_out=ssq[:, p:p + 1]).then_inc(ctx_sq, 1)
                    if r == R_KTURN:
                        act.wait_ge(k_turned, n)
                        if isinstance(A, int) and c == 0:
                            act.wait_ge(diag_zero, 2)
                        for g in range(NG):
                            d = slice(HD * g, HD * g + HD)
                            last = act.activation(kD_hi[d, g, :], pvb[d, 0:P], ACT.Copy)
                        last.then_inc(k_high, 1)
                    if r in R_PT:
                        m = r - R_PT[0]
                        act.wait_ge(probs_turned, 4 * (n - 1) + m + 1)
                        act.activation(prT[:, :, m, :], tb[m % 2][:].rearrange("p (g t) -> p g t", g=NG),
                                       ACT.Copy).then_inc(probsT, 1)
                    if r == R_PV:
                        act.wait_ge(heads_out, n)
                        act.activation(oT_hi[:].rearrange("p n t -> p (n t)"), pvb[:], ACT.Copy).then_inc(o_high, 1)
                    if s == TURN2[c]:
                        act.wait_ge(xn2_turned, n)
                        act.activation(xnT_hi[:, :, P * c:P * c + P], prb[:].rearrange("p (k t) -> p k t", k=KC),
                                       ACT.Copy, scale=XN_SCALE).then_inc(xn_high, 1)
            def hidden(F, h):
                act.wait_ge(up_done, 16 * F + h + 1)
                if h >= 2:
                    act.wait_ge(x2_low, 16 * F + h - 1)
                act.activation(relu[:, h % 2, :], ff[h % 2][:], ACT.Relu, bias=b_up[:, h:h + 1],
                               scale=su[:]).then_inc(relu_done, 1)
                act.wait_ge(relu_done, 16 * F + h + 1)
                act.activation(x2_hi[:, h, :], relu[:, h % 2, :], ACT.Copy).then_inc(x2_high, 1)

            def store(F, t):
                act.wait_ge(down_read, 4 * F + 4 + t + 1)
                act.dma_start(out_v[4 * F + t], y[:, t, :]).then_inc(y_free[t], 16)

            def feed_forward(F, s):
                if 1 <= s <= 16:
                    hidden(F, s - 1)
                if s in (20, 24, 28):
                    store(F, (s - 20) // 4)

            for s in range(SLOTS + LAG + 1):
                if s == 2:
                    lora_copy()
                if s < SLOTS:
                    exponentials(0, s)
                if s > LAG:
                    weights(s - LAG - 1)
                if s < SLOTS:
                    attention(0, s)
                if s == 0:
                    act.wait_ge(consts_in, 16)
                    act.activation(ident16[:], ident, ACT.Copy).then_inc(ident_cast, 1)
                if s == 1:
                    lora_high()
                if s == 2:
                    order_wout()
                if WOUT_AT < s <= WOUT_AT + NN:
                    wout_high(s - WOUT_AT - 1)
            act.wait_ge(bias_scaled, 1)
            with act.Fori(0, NBLK - 1) as i:
                for s in range(SLOTS):
                    feed_forward(i, s)
                    exponentials(i + 1, s)
                    attention(i + 1, s)
                store(i, 3)
            for s in range(SLOTS):
                feed_forward(NBLK - 1, s)
            store(NBLK - 1, 3)
            for t in range(BPB):
                act.wait_ge(y_free[t], 16 * NBLK + 16)

        @block.tensor
        def _(pe):
            def turn(dst, src, **kw):
                return pe.matmul(dst, src, ident[0:src.shape[0], 0:src.shape[0]], is_transpose=True, **kw)

            def wout_turn(m):
                if m == 0:
                    pe.wait_ge(consts_in, 16)
                    pe.wait_ge(wo_ordered, KC)
                if m >= 2:
                    pe.wait_ge(wo_low, m - 1)
                for j in range(KC):
                    last = turn(tb[m % 2][:, P * j:P * j + P], wo_nat[:, j, P * m:P * m + P], start=True, stop=True)
                last.then_inc(wo_turned, 1)

            def lora_turn():
                pe.wait_ge(ident_cast, 1)
                pe.wait_ge(a_high, 2)
                pe.wait_ge(a_low, 2)
                for i, chunks in enumerate((range(0, 4), range(4, 12), range(12, 20))):
                    if i == 2:
                        pe.wait_ge(a_copied, 1)
                    for j, b in enumerate(chunks):
                        last = pe.transpose(ff[i % 2][0:R3, 64 * j:64 * j + 64].bitcast(F16),
                                            a_parts[:, b].rearrange("p k r -> p (k r)"), ident16[:])
                    last.then_inc(a_turned, 1)

            def weights(s):
                if s < 2:
                    pe.wait_ge(a_copied, 3)
                elif s < 30:
                    pe.wait_ge(w_low, s - 1)
                else:
                    pe.wait_ge(down_read, s - 29)
                g, j = divmod(s, 4)
                if s in (0, 4):
                    pe.wait_ge(b_high, 1 if s == 0 else 3)
                    pe.wait_ge(b_low, 1 if s == 0 else 3)
                if s < 16:
                    a, b = a_up3[:, P * j:P * j + P], b_up3[:, 512 * g:512 * g + 512]
                else:
                    a, b = a_dn3[:, P * (s - 16):P * (s - 16) + P], b_dn3[:]
                lora = pe.matmul(ff[s % 2][:], a, b, start=True, stop=False, skip_group_check=True)
                if 8 <= s < 8 + BPB:
                    lora.then_inc(y_free[s - 8], 16)
                if j == 0:
                    pe.wait_ge(deq_v, 2 * g + 2)
                    pe.wait_ge(deq_g, 2 * g + 2)
                for t in range(4):
                    last = turn(ff[s % 2][:, P * t:P * t + P], stage[:, g % 4, t, P * j:P * j + P],
                                start=False, stop=(t == 3), skip_group_check=True)
                last.then_inc(w_turned, 1)

            def attention(A, s):
                for c in range(BPB):
                    r = s - BASE[c]
                    n = 4 * A + c + 1
                    if r in R_PT:
                        m = r - R_PT[0]
                        pe.wait_ge(probs, 4 * (n - 1) + m + 1)
                        if isinstance(A, int) and c == 0 and m < 2:
                            pe.wait_ge(wo_low, NN - 1 + m)
                        after(pe, probsT, 4 * (n - 1) + m - 1)
                        for g in range(NG):
                            last = turn(tb[m % 2][:, P * g:P * g + P], pr[:, m, g, :], start=True, stop=True)
                        last.then_inc(probs_turned, 1)
                for c in range(BPB):
                    r = s - BASE[c]
                    n = 4 * A + c + 1
                    if r == R_KTURN:
                        pe.wait_ge(k_ready, n)
                        if isinstance(A, int) and c == 0:
                            pe.wait_ge(consts_in, 16)
                        after(pe, o_low, 4 * A + before(PV_AT, s))
                        turn(pvb[:, 0:P], k[:], start=True, stop=True).then_inc(k_turned, 1)
                    if r == R_PV:
                        pe.wait_ge(probsT, 4 * n)
                        after(pe, o_low, n - 1)
                        for g in range(NG):
                            d = slice(HD * g, HD * g + HD)
                            last = pe.matmul(pvb[d, :], kvt[:, c, d], prT[:, g].rearrange("p n t -> p (n t)"),
                                             start=True, stop=True)
                        last.then_inc(heads_out, 1)
                    if r == R_PROJ:
                        pe.wait_ge(o_low, n)
                        after(pe, x1_ready, n - 1)
                        after(pe, xn_low, 4 * A + before(TURN2, s))
                        if isinstance(A, int) and c == 0:
                            pe.wait_ge(wo_low, NN)
                        terms = ((oT_hi, wo_hi), (oT_lo, wo_hi), (oT_hi, wo_lo))
                        for i, (a, b) in enumerate(terms):
                            for m in range(NN):
                                last = pe.matmul(prb[:], a[:, m, :], b[:, m, :],
                                                 start=(i == 0 and m == 0), stop=(i == 2 and m == NN - 1))
                        last.then_inc(projected, 1)
                    if s == TURN2[c]:
                        pe.wait_ge(xn2_ready, n)
                        after(pe, x1_ready, 4 * A + before(PROJ_AT, s))
                        after(pe, xn_low, n - 1)
                        for m in range(KC):
                            last = turn(prb[:, P * m:P * m + P], xn2[:, c % 2, P * m:P * m + P], start=True, stop=True)
                        last.then_inc(xn2_turned, 1)

            def attention_end(A, s):
                for c in range(BPB):
                    r = s - BASE[c]
                    n = 4 * A + c + 1
                    if r in R_SCORES:
                        m = r - R_SCORES[0]
                        if m == 0:
                            pe.wait_ge(q_low, n)
                            pe.wait_ge(k_low, n)
                            if isinstance(A, int) and c == 0:
                                pe.wait_ge(bias_scaled, 1)
                        after(pe, masked, 4 * (n - 1) + m - 1)
                        terms = ((qT_hi, kD_hi), (qT_lo, kD_hi), (qT_hi, kD_lo))
                        for i, (a, b) in enumerate(terms):
                            last = pe.matmul(sbk[m % 2][:], a[:, m, :], b[:].rearrange("p g t -> p (g t)"),
                                             start=(i == 0), stop=(i == 2))
                        last.then_inc(scores, 1)
                for c in range(BPB):
                    r = s - BASE[c]
                    n = 4 * A + c + 1
                    if r == R_QTURN:
                        pe.wait_ge(q_ready, n)
                        after(pe, x1_ready, 4 * A + before(PROJ_AT, s, itself=True))
                        after(pe, xn_low, 4 * A + before(TURN2, s, itself=True))
                        for m in range(NN):
                            last = turn(prb[:, P * m:P * m + P], q[:, P * m:P * m + P], start=True, stop=True)
                        last.then_inc(q_turned, 1)

            def feed_forward(F, s):
                if s < HC:
                    if s == 0:
                        pe.wait_ge(xn_low, 4 * F + 4)
                    if s < 2:
                        pe.wait_ge(down_read, 4 * F + 3 + s)
                    else:
                        pe.wait_ge(relu_done, 16 * F + s - 1)
                    terms = ((wu_hi, xnT_hi), (wu_hi, xnT_lo), (wu_lo, xnT_hi))
                    for m in range(KC):
                        for i, (a, b) in enumerate(terms):
                            last = pe.matmul(ff[s % 2][:], a[:, m, P * s:P * s + P], b[:, m, :],
                                             start=(m == 0 and i == 0), stop=(m == KC - 1 and i == 2))
                    last.then_inc(up_done, 1)
                else:
                    t, part = divmod(s - HC, 4)
                    if part == 0:
                        if t < 2:
                            pe.wait_ge(relu_done, 16 * F + 15 + t)
                        else:
                            pe.wait_ge(down_read, 4 * F + 4 + t - 1)
                    terms = ((x2_hi, wd_hi), (x2_lo, wd_hi), (x2_hi, wd_lo))
                    for h in range(4 * part, 4 * part + 4):
                        if t == 0:
                            pe.wait_ge(x2_low, 16 * F + h + 1)
                        for i, (a, b) in enumerate(terms):
                            last = pe.matmul(ff[t % 2][:], a[:, h, P * t:P * t + P], b[:, h, :],
                                             start=(h == 0 and i == 0), stop=(h == HC - 1 and i == 2))
                    if part == 3:
                        last.then_inc(down_done, 1)

            for s in range(SLOTS + LAG):
                if s < SLOTS:
                    attention(0, s)
                if s == 0:
                    pe.wait_ge(consts_in, 16)
                    pe.wait_ge(scales_in, 16 * 5)
                    turn(sbk[0][:, 0:HC], b_nat[:], start=True, stop=True).then_inc(b_turned, 1)
                if s == 1:
                    lora_turn()
                if s >= LAG:
                    weights(s - LAG)
                if WOUT_AT <= s < WOUT_AT + NN:
                    wout_turn(s - WOUT_AT)
                if s < SLOTS:
                    attention_end(0, s)
            pe.wait_ge(w_low, 28)
            pe.wait_ge(down_read, 4)
            with pe.Fori(0, NBLK - 1) as i:
                for s in range(SLOTS):
                    attention(i + 1, s)
                    feed_forward(i, s)
                    attention_end(i + 1, s)
            for s in range(SLOTS):
                feed_forward(NBLK - 1, s)

        @block.vector
        def _(dve):
            step = [0]

            def link(ins, wait=True):
                step[0] += 1
                ins.then_inc(scale_steps, 1)
                if wait:
                    dve.wait_ge(scale_steps, step[0])

            def find_tops():
                dve.memset(tops[:], 0.0).then_inc(tops_zero, 1)
                dve.wait_ge(tops_zero, 1)
                dve.wait_ge(scales_in, 16 * 5)
                dve.wait_ge(b_flat_in, 16 * 2)
                for j, v in enumerate((s_up[:].rearrange("p a b -> p (a b)"), s_dn[:].rearrange("p a b -> p (a b)"),
                                       a_nat[:, 0:KC * R], a_nat[:, KC * R:], b_up_flat, b_dn_flat, b_nat[:])):
                    dve.tensor_reduce(tops[0:v.shape[0], j:j + 1], v, AXX, ALU.max,
                                      apply_absolute_value=True).then_inc(tops_ready, 1)

            def find_scales():
                dve.wait_ge(tops_reduced, 1)
                lora, deq, wtop, wpow, ytop, atop, apow = (tmp[:, 2 * i:2 * i + 2] for i in range(7))
                link(dve.tensor_tensor(lora, tops_all[:, 2:4], tops_all[:, 4:6], ALU.mult), wait=False)
                link(dve.tensor_scalar(deq, tops_all[:, 0:2], 7.5, 1e-30, ALU.mult, ALU.add), wait=False)
                link(dve.tensor_scalar(atop, tops_all[:, 2:4], 1e-30, None, ALU.add))
                link(dve.scalar_tensor_tensor(wtop, lora, float(R), deq, ALU.mult, ALU.add))
                link(dve.scalar_tensor_tensor(ytop[:, 0:1], wtop[:, 0:1], float(C), tops_all[:, 6:7], ALU.mult, ALU.add))
                for dst, src, wait in ((wpow, wtop, False), (apow, atop, False), (ytop[:, 1:2], ytop[:, 0:1], True)):
                    link(dve.tensor_scalar(dst.bitcast(I32), src.bitcast(I32), 0x7F800000, None, ALU.bitwise_and), wait)
                link(dve.reciprocal(kap[:, 0:2], wpow), wait=False)
                link(dve.reciprocal(kap[:, 2:4], apow), wait=False)
                link(dve.reciprocal(kap[:, 6:7], ytop[:, 1:2]))
                link(dve.tensor_scalar(kap[:, 0:2], kap[:, 0:2], W_TOP, None, ALU.mult), wait=False)
                link(dve.tensor_scalar(kap[:, 2:4], kap[:, 2:4], A_TOP, None, ALU.mult), wait=False)
                link(dve.tensor_scalar(kap[:, 6:7], kap[:, 6:7], X2_TOP, None, ALU.mult))
                link(dve.scalar_tensor_tensor(kap[:, 4:6], kap[:, 0:2], 1.0 / A_TOP, apow, ALU.mult, ALU.mult), wait=False)
                link(dve.tensor_scalar(su[:], wpow[:, 0:1], kap[:, 6:7], 1.0 / (W_TOP * XN_SCALE), ALU.mult, ALU.mult), wait=False)
                link(dve.tensor_scalar(sd[:], wpow[:, 1:2], ytop[:, 1:2], 1.0 / (W_TOP * X2_TOP), ALU.mult, ALU.mult), wait=False)
                for v, kx in ((s_up[:], kap[:, 0:1]), (s_dn[:], kap[:, 1:2])):
                    dve.tensor_scalar(v, v, kx, None, ALU.mult).then_inc(scales_ready, 1)
                assert step[0] == SCALE_STEPS
                dve.wait_ge(scales_ready, 2)

            def lora_a_low():
                dve.wait_ge(a_high, 2)
                for cols, chunks, kx in ((slice(0, KC * R), slice(0, KC), 2), (slice(KC * R, None), slice(KC, None), 3)):
                    dve.scalar_tensor_tensor(a_parts[:, chunks, 1, :], a_nat[:, cols].rearrange("p (c r) -> p c r", r=R),
                                             kap[:, kx:kx + 1], a_parts[:, chunks, 0, :],
                                             ALU.mult, ALU.subtract).then_inc(a_low, 1)

            def lora_b_low():
                rows = slice(2 * R, R3)
                for i, (dst, src, kx) in enumerate(b_pieces):
                    dve.wait_ge(b_high, i + 1)
                    dve.scalar_tensor_tensor(dst[rows], src[rows], kap[rows, kx:kx + 1], dst[rows],
                                             ALU.mult, ALU.subtract).then_inc(b_low, 1)

            def wout_low(m):
                dve.wait_ge(wo_high, m + 1)
                dve.tensor_tensor(wo_lo[:, m, :], tb[m % 2][:], wo_hi[:, m, :].bitcast(F32),
                                  ALU.subtract).then_inc(wo_low, 1)

            def dequant(t):
                g, j = divmod(t, 4)
                dve.wait_ge(wq_in[g % 4], 16 * (g // 4 + 1))
                dve.scalar_tensor_tensor(stage[:, g % 4, j, :].rearrange("p (b c) -> p b c", c=QB),
                                         stage_i[:, g % 4, j, :].rearrange("p (b c) -> p b c", c=QB), -7.5,
                                         scale_of(t), ALU.add, ALU.mult).then_inc(deq_v, 1)

            def weights(s):
                dve.wait_ge(w_high, s + 1)
                cols = slice(512 * (s // 4), 512 * (s // 4) + 512)
                hi, lo = ((wu_hi[:, s % 4, cols], wu_lo[:, s % 4, cols]) if s < 16 else
                          (wd_hi[:, s - 16, :], wd_lo[:, s - 16, :]))
                dve.tensor_tensor(lo, ff[s % 2][:], hi, ALU.subtract).then_inc(w_low if s < 28 else down_read, 1)

            def inverse_sums(A, s):
                for c in range(BPB):
                    r = s - BASE[c]
                    n = 4 * A + c + 1
                    p = c % 2
                    if r in R_PROBS:
                        m = r - R_PROBS[0]
                        dve.wait_ge(exps, 4 * (n - 1) + m + 1)
                        dve.reciprocal(rinv[:, p, 4 * m:4 * m + 4], rsum[:, p, 4 * m:4 * m + 4]).then_inc(inv_sums, 1)

            def attention_early(A, s):
                for c in range(BPB):
                    r = s - BASE[c]
                    n = 4 * A + c + 1
                    p = c % 2
                    if r == R_STATS:
                        dve.wait_ge(x_in[c], 16 * A + 16)
                        dve.bn_stats(stats[:, p, :], xt[:, c, :]).then_inc(x_stats, 1)
                    if r == R_CENTRE:
                        dve.wait_ge(norms, n)
                        after(dve, q_cos, n - 1)
                        dve.tensor_scalar(xc[:], xt[:, c, :], mv[:, p, 0:1], inv[:, p, 0:1],
                                          ALU.subtract, ALU.mult).then_inc(x_centred, 1)
                        dve.wait_ge(x_centred, n)
                        if isinstance(A, int) and c == 0:
                            dve.wait_ge(tables_ready, 4)
                        dve.tensor_tensor(halves(t_sin[:], False), halves(xc[:], True), halves(sw[:], False),
                                          ALU.mult).then_inc(q_sin, 1)
                    if r == R_ROPE:
                        dve.wait_ge(q_cos, n)
                        dve.wait_ge(q_sin, n)
                        after(dve, q_turned, n - 1)
                        dve.tensor_tensor(q[:].rearrange("p (n g d) -> p g n d", g=NG, d=HD),
                                          t_cos[:].rearrange("p (g n d) -> p g n d", g=NG, d=HD),
                                          t_sin[:].rearrange("p (g n d) -> p g n d", g=NG, d=HD),
                                          ALU.add).then_inc(q_ready, 1)
                    if r == R_X1:
                        dve.wait_ge(projected, n)
                        after(dve, y_base, n - 4)
                        dve.tensor_tensor(x1[:, c, :], prb[:], xt[:, c, :], ALU.add).then_inc(x1_ready, 1)
                        dve.wait_ge(x1_ready, n)
                        dve.bn_stats(stats2[:, p, :], x1[:, c, :]).then_inc(x1_stats, 1)
                        dve.wait_ge(x1_stats, n)
                        dve.memset(spare[:], 0.0)
                        dve.bn_aggr(mv2[:, p, :], stats2[:, p, :]).then_inc(x1_moments, 1)
                        dve.wait_ge(x1_moments, n)
                        dve.tensor_scalar(arg2[:, p:p + 1], mv2[:, p, 1:2], EPS, None, ALU.add).then_inc(arg2_ready, 1)
                for c in range(BPB):
                    r = s - BASE[c]
                    n = 4 * A + c + 1
                    p = c % 2
                    if r in R_MASK:
                        m = r - R_MASK[0]
                        dve.wait_ge(scores, 4 * (n - 1) + m + 1)
                        dve.scalar_tensor_tensor(pr[:, m], sbk[m % 2][:].rearrange("p (g t) -> p g t", g=NG), -SC,
                                                 mask.unsqueeze(1).broadcast_to([P, NG, P]),
                                                 ALU.mult, ALU.add).then_inc(masked, 1)
                        dve.wait_ge(masked, 4 * (n - 1) + m + 1)
                        dve.tensor_reduce(nmax[:, p, 4 * m:4 * m + 4], pr[:, m], AXX, ALU.min).then_inc(row_max, 1)
                for c in range(BPB):
                    r = s - BASE[c]
                    n = 4 * A + c + 1
                    if r == R_QSPLIT:
                        dve.wait_ge(q_high, n)
                        dve.tensor_tensor(qT_lo[:].rearrange("p n t -> p (n t)"), prb[:],
                                          qT_hi[:].rearrange("p n t -> p (n t)").bitcast(F32),
                                          ALU.subtract).then_inc(q_low, 1)

            def attention_late(A, s):
                for c in range(BPB):
                    r = s - BASE[c]
                    n = 4 * A + c + 1
                    p = c % 2
                    if r == R_STATS:
                        dve.wait_ge(ctx_sq, n)
                        dve.wait_ge(x_stats, n)
                        dve.tensor_scalar(arg[:, p, 1:2], ssq[:, p:p + 1], 1.0 / CK, EPS,
                                          ALU.mult, ALU.add).then_inc(norm_args, 1)
                        dve.bn_aggr(mv[:, p, :], stats[:, p, :]).then_inc(x_moments, 1)
                        dve.wait_ge(x_moments, n)
                        dve.tensor_scalar(arg[:, p, 0:1], mv[:, p, 1:2], 1.0 + EPS, EPS * EPS,
                                          ALU.mult, ALU.add).then_inc(norm_args, 1)
                    if r == R_KTURN:
                        dve.wait_ge(k_high, n)
                        if isinstance(A, int) and c == 0:
                            dve.wait_ge(diag_zero, 2)
                        for g in range(NG):
                            d = slice(HD * g, HD * g + HD)
                            last = dve.tensor_tensor(kD_lo[d, g, :], pvb[d, 0:P], kD_hi[d, g, :].bitcast(F32),
                                                     ALU.subtract)
                        last.then_inc(k_low, 1)
                    if r == R_PV:
                        dve.wait_ge(o_high, n)
                        dve.tensor_tensor(oT_lo[:].rearrange("p n t -> p (n t)"), pvb[:],
                                          oT_hi[:].rearrange("p n t -> p (n t)").bitcast(F32),
                                          ALU.subtract).then_inc(o_low, 1)
                    if r == R_NORM2:
                        dve.wait_ge(norm2, n)
                        after(dve, xn2_turned, n - 2)
                        dve.tensor_scalar(xn2[:, p, :], x1[:, c, :], mv2[:, p, 0:1], inv2[:, p:p + 1],
                                          ALU.subtract, ALU.mult).then_inc(xn2_ready, 1)
                    if s == TURN2[c]:
                        dve.wait_ge(xn_high, n)
                        dve.scalar_tensor_tensor(xnT_lo[:, :, P * c:P * c + P], prb[:].rearrange("p (k t) -> p k t", k=KC),
                                                 XN_SCALE, xnT_hi[:, :, P * c:P * c + P],
                                                 ALU.mult, ALU.subtract).then_inc(xn_low, 1)

            def result(F, t):
                dve.wait_ge(down_done, 4 * F + t + 1)
                dve.wait_ge(y_base, 4 * F + t + 1)
                dve.scalar_tensor_tensor(y[:, t, :], ff[t % 2][:], sd[:], y[:, t, :],
                                         ALU.mult, ALU.add).then_inc(down_read, 1)

            def x2_lows(F, s):
                if 1 <= s <= 16:
                    h = s - 1
                    dve.wait_ge(x2_high, 16 * F + h + 1)
                    dve.tensor_tensor(x2_lo[:, h, :], relu[:, h % 2, :], x2_hi[:, h, :], ALU.subtract).then_inc(x2_low, 1)

            for s in range(SLOTS + LAG + 2):
                if s < SLOTS:
                    inverse_sums(0, s)
                if s == 1:
                    find_scales()
                    dequant(0)
                    lora_a_low()
                    dve.wait_ge(b_turned, 1)
                    dve.tensor_scalar(b_up[:], sbk[0][:, 0:HC], kap[:, 6:7], None, ALU.mult).then_inc(bias_scaled, 1)
                if s > LAG + 1:
                    weights(s - LAG - 2)
                for t in tiles_to_dequantise(s):
                    if t % 2 == 0 and t > 0:
                        dequant(t)
                if s < SLOTS:
                    attention_early(0, s)
                    attention_late(0, s)
                if s == 0:
                    find_tops()
                if s == 1:
                    lora_b_low()
                if WOUT_AT < s <= WOUT_AT + NN:
                    wout_low(s - WOUT_AT - 1)
            with dve.Fori(0, NBLK - 1) as i:
                for s in range(SLOTS):
                    if s in (20, 24, 28):
                        result(i, (s - 20) // 4)
                    inverse_sums(i + 1, s)
                    attention_early(i + 1, s)
                    x2_lows(i, s)
                    attention_late(i + 1, s)
                result(i, 3)
            for s in range(SLOTS):
                if s in (20, 24, 28):
                    result(NBLK - 1, (s - 20) // 4)
                x2_lows(NBLK - 1, s)
            result(NBLK - 1, 3)


_INS = ["x", "ctx_512", "L0_xattn_q_norm_w", "L0_xattn_k_norm_w", "L0_xattn_w_out",
        "L0_ffn_w_up_q", "L0_ffn_w_up_scale", "L0_ffn_b_up", "L0_ffn_w_up_lora_a", "L0_ffn_w_up_lora_b",
        "L0_ffn_w_down_q", "L0_ffn_w_down_scale", "L0_ffn_b_down", "L0_ffn_w_down_lora_a", "L0_ffn_w_down_lora_b"]


def shape_tables(T=128, HD=32, theta=10000.0):
    f = np.float32
    inv_freq = f(1.0) / np.power(f(theta), np.arange(0, HD, 2, dtype=f) / f(HD)).astype(f)
    freqs = np.outer(np.arange(T, dtype=f), inv_freq).astype(f)
    emb = np.concatenate([freqs, freqs], -1)
    sin = np.sin(emb).astype(f)
    sin[:, :HD // 2] *= f(-1.0)
    causal = np.where(np.tril(np.ones((T, T), bool)), f(0), f(BIG)).astype(f)
    return {"tables": np.concatenate([np.eye(T, dtype=f), causal, np.cos(emb).astype(f), sin], 1)}


def kernel(**inputs):
    import concourse.bacc as _bacc
    from concourse import mybir as _mybir
    from concourse.bass_utils import run_bass_kernel_spmd as _run

    nc = _bacc.Bacc("TRN2", target_bir_lowering=False, num_devices=1)
    arrays, args = {}, []
    for name, a in [(n, inputs[n]) for n in _INS] + list(shape_tables().items()):
        a = np.ascontiguousarray(a)
        arrays[f"in_{name}"] = a
        args.append(nc.dram_tensor(f"in_{name}", a.shape, _mybir.dt.from_np(a.dtype), kind="ExternalInput").ap())
    args.append(nc.dram_tensor("out_0", tuple(inputs["x"].shape), _mybir.dt.float32, kind="ExternalOutput").ap())
    build(nc, *args)
    r = _run(nc, [arrays], core_ids=[0])
    return r.results[0]["out_0"]
```

```python
from contextlib import ExitStack

import concourse.bass as bass
import numpy as np
from concourse import mybir

F32 = mybir.dt.float32
F32R = mybir.dt.float32r
F16 = mybir.dt.float16
I32 = mybir.dt.int32
ALU = mybir.AluOpType
ACT = mybir.ActivationFunctionType
AXX = mybir.AxisListType.X

P = 128
EPS = 1e-5
SCALE_STEPS = 17
XN_SCALE = 1024.0
Q_TOP, K_TOP = 2.0 ** 10, 2.0 ** 11
W_TOP, A_TOP, X2_TOP = 2.0 ** 13, 2.0 ** 10, 2.0 ** 14
BIG = 1e30

BPB = 4
SLOTS = 32
BASE = (0, 5, 11, 16)
R_STATS, R_CENTRE, R_ROPE = 0, 1, 2
R_KSPLIT, R_KTURN, R_KTAKE = 1, 2, 3
R_QSPLIT = 2
R_QTURN = 3
R_QTAKE = (3, 4)
R_SCORES = (3, 4, 5, 6)
R_MASK = (4, 5, 6, 7)
R_EXP = (5, 6, 7, 8)
R_PROBS = (6, 7, 8, 9)
R_PT = (7, 8, 9, 10)
R_PV, R_PROJ, R_X1, R_NORM2 = 11, 12, 13, 14
TURN2 = (21, 25, 27, 31)
WOUT_AT = 3
DVE_TILES = (0, 2, 4, 6, 8, 12, 16, 20, 24, 28)
DEQ_LEAD = 4
RESIDUAL_AT = (3, 4, 9, 10)
LAG = 3


def build(nc, x, ctx, qw, kw, wo, wuq, wus, bu, wua, wub, wdq, wds, bd, wda, wdb,
          tabs_d, out):
    B, T, C = x.shape
    CK = ctx.shape[2]
    HD, NG = 32, 4
    NN = C // HD // NG
    H = wuq.shape[0]
    R = wua.shape[1]
    KC, HC = C // P, H // P
    NBLK = B // BPB
    QB = 64
    SC = float(np.float32(1.0) / np.sqrt(np.float32(HD)))
    assert T == P and CK == P and NBLK == 4 and HC == 16 and KC == 4 and NN == 4

    with ExitStack() as es:
        def sb(name, shape, dt=F32):
            return es.enter_context(nc.sbuf_tensor(name, shape, dt))

        def sem(name):
            return es.enter_context(nc.semaphore(name))

        wu_hi, wu_lo = sb("wu_hi", [P, KC, H], F16), sb("wu_lo", [P, KC, H], F16)
        wd_hi, wd_lo = sb("wd_hi", [P, HC, C], F16), sb("wd_lo", [P, HC, C], F16)
        wo_hi, wo_lo = sb("wo_hi", [P, NN, C], F32R), sb("wo_lo", [P, NN, C], F32R)
        xnT_hi, xnT_lo = sb("xnT_hi", [P, KC, BPB * P], F16), sb("xnT_lo", [P, KC, BPB * P], F16)
        big = sb("big", [P, 8192])
        x2_hi = big[:, 0:4096].bitcast(F16).rearrange("p (h t) -> p h t", h=HC)
        x2_lo = big[:, 4096:8192].bitcast(F16).rearrange("p (h t) -> p h t", h=HC)
        stage = big[:].rearrange("p (b j c) -> p b j c", b=4, j=4)
        stage_i = big[:].bitcast(I32).rearrange("p (b j c) -> p b j c", b=4, j=4)
        low_area = wd_lo[:].rearrange("p h c -> p (h c)").bitcast(F32)
        high_area = wd_hi[:].rearrange("p h c -> p (h c)").bitcast(F32)
        wo_raw = low_area[:, 0:2048].rearrange("p (j c) -> p j c", c=C)
        a_nat = low_area[:, 3072:3072 + (KC + HC) * R]
        a_parts = (low_area[:, 3392:3392 + (KC + HC) * R * 3 // 2].bitcast(F16)
                   .rearrange("p (c k r) -> p c k r", k=3, r=R))
        b_up_flat = high_area[:, 2048:2048 + R * H // P]
        b_dn_flat = high_area[:, 2304:2304 + R * C // P]
        qw_bc, kw_bc = high_area[:, 2368:2368 + C], high_area[:, 2880:2880 + CK]
        relu = sb("relu", [P, 2, BPB * P])
        R3 = 3 * R
        b_up_in, b_dn_in = high_area[0:R3, 0:H], high_area[0:R3, 3072:3072 + C]
        b_up3 = low_area[0:R3, 2048:3072].bitcast(F16)
        a_dn3 = relu[0:R3].rearrange("p a b -> p (a b)").bitcast(F16)
        a_up3, b_dn3 = sb("a_up3", [R3, C], F16), sb("b_dn3", [R3, C], F16)
        xt = sb("xt", [P, BPB, C])
        x1 = sb("x1", [P, BPB, C])
        y = sb("y", [P, BPB, C])
        kvt = sb("kvt", [P, BPB, CK])
        cw, sw = sb("cw", [P, C]), sb("sw", [P, C])
        cwk, swk = sb("cwk", [P, CK]), sb("swk", [P, CK])
        tabs = sb("tabs", [P, 2 * P + 2 * HD])
        ident, mask = tabs[:, 0:P], tabs[:, P:2 * P]
        cos_s, sin_s = tabs[:, 2 * P:2 * P + HD], tabs[:, 2 * P + HD:]
        bd_bc = sb("bd_bc", [P, C])
        xc = sb("xc", [P, C])
        t_cos, t_sin, q = sb("t_cos", [P, C]), sb("t_sin", [P, C]), sb("q", [P, C])
        k_cos, k_sin, k_sum, k = (sb(s, [P, CK]) for s in ("k_cos", "k_sin", "k_sum", "k"))
        sq_junk = sb("sq_junk", [P, CK])
        HD3 = 3 * HD
        q3, k3 = sb("q3", [P, NN * NG, 3, HD], F16), sb("k3", [P, NG, 3, HD], F16)
        qT, kT = sb("qT", [HD3, NN * NG, P], F16), sb("kT", [HD3, NG, P], F16)
        pr = sb("pr", [P, NN, NG, P])
        prT = sb("prT", [P, NG, NN, P])
        ident16 = sb("ident16", [P, P], F16)
        b_nat = sb("b_nat", [HC, P])
        oT_hi, oT_lo = sb("oT_hi", [P, NN, P], F32R), sb("oT_lo", [P, NN, P], F32R)
        xn2 = sb("xn2", [P, 2, C])
        stats, stats2 = sb("stats", [P, 2, 6]), sb("stats2", [P, 2, 6])
        spare = sb("spare", [P, 1])
        mv, mv2 = sb("mv", [P, 2, 2]), sb("mv2", [P, 2, 2])
        ssq = sb("ssq", [P, 2])
        arg, inv = sb("arg", [P, 2, 2]), sb("inv", [P, 2, 2])
        arg2, inv2 = sb("arg2", [P, 2]), sb("inv2", [P, 2])
        minus_half = sb("minus_half", [P, 2])
        nmax = sb("nmax", [P, 2, NN * NG])
        rsum, rinv = sb("rsum", [P, 2, NN * NG]), sb("rinv", [P, 2, NN * NG])
        s_up, s_dn = sb("s_up", [P, HC, C // QB]), sb("s_dn", [P, KC, H // QB])
        b_up = sb("b_up", [P, HC])
        tops, tops_all = sb("tops", [P, 8]), sb("tops_all", [P, 8])
        tmp = sb("tmp", [P, 16])
        kap = sb("kap", [P, 8])
        su, sd = sb("su", [P, 1]), sb("sd", [P, 1])
        wmax, wpow2, wsq = sb("wmax", [P, 2]), sb("wpow2", [P, 2]), sb("wsq", [P, 2])
        arg_mul, arg_add, score_scale = sb("arg_mul", [P, 2]), sb("arg_add", [P, 2]), sb("score_scale", [P, 1])

        def bank(name):
            return es.enter_context(nc.psum_tensor(name, [P, 512], F32))
        ff = [bank("ff0"), bank("ff1")]
        sbk = [bank("sb0"), bank("sb1")]
        tb = [bank("tb0"), bank("tb1")]
        pvb = bank("pvb")
        prb = bank("prb")

        prb16, pvb16 = prb[:].bitcast(F16), pvb[:].bitcast(F16)

        norm_w_in = sem("norm_w_in")
        consts_in, scales_in, wout_in = sem("consts_in"), sem("scales_in"), sem("wout_in")
        b_in = sem("b_in")
        wq_in = [sem(f"wq_in{i}") for i in range(4)]
        down_bias_in, b_flat_in = sem("down_bias_in"), sem("b_flat_in")
        x_in = [sem(f"x_in{i}") for i in range(BPB)]
        kv_in = [sem(f"kv_in{i}") for i in range(BPB)]
        y_free = [sem(f"y_free{i}") for i in range(BPB)]
        tops_zero, tops_ready, tops_reduced = sem("tops_zero"), sem("tops_ready"), sem("tops_reduced")
        scale_steps, scales_ready = sem("scale_steps"), sem("scales_ready")
        tables_ready, pool_consts = sem("tables_ready"), sem("pool_consts")
        norm_scale_steps = sem("norm_scale_steps")
        bias_scaled = sem("bias_scaled")
        a_high, a_low, b_high, b_low = sem("a_high"), sem("a_low"), sem("b_high"), sem("b_low")
        ident_cast, b_turned = sem("ident_cast"), sem("b_turned")
        a_turned, a_copied = sem("a_turned"), sem("a_copied")
        wo_ordered = sem("wo_ordered")
        wo_turned, wo_high, wo_low = sem("wo_turned"), sem("wo_high"), sem("wo_low")
        deq_v, deq_g, deq_g1 = sem("deq_v"), sem("deq_g"), sem("deq_g1")
        w_turned, w_high, w_low = sem("w_turned"), sem("w_high"), sem("w_low")
        x_stats, x_moments, ctx_sq = sem("x_stats"), sem("x_moments"), sem("ctx_sq")
        norm_args, norms = sem("norm_args"), sem("norms")
        x_centred, q_cos, q_sin, q_ready = sem("x_centred"), sem("q_cos"), sem("q_sin"), sem("q_ready")
        k_parts, k_summed, k_ready = sem("k_parts"), sem("k_summed"), sem("k_ready")
        q_turned, k_turned = sem("q_turned"), sem("k_turned")
        q_high, q_low, k_high, k_low = sem("q_high"), sem("q_low"), sem("k_high"), sem("k_low")
        q_taken0, q_taken1, k_taken = sem("q_taken0"), sem("q_taken1"), sem("k_taken")
        scores, masked, row_max = sem("scores"), sem("masked"), sem("row_max")
        exps, inv_sums, probs = sem("exps"), sem("inv_sums"), sem("probs")
        probs_turned, probsT = sem("probs_turned"), sem("probsT")
        heads_out, o_high, o_low = sem("heads_out"), sem("o_high"), sem("o_low")
        projected, x1_ready = sem("projected"), sem("x1_ready")
        x1_stats, x1_moments, arg2_ready, norm2 = sem("x1_stats"), sem("x1_moments"), sem("arg2_ready"), sem("norm2")
        xn2_ready, xn2_turned, xn_high, xn_low = sem("xn2_ready"), sem("xn2_turned"), sem("xn_high"), sem("xn_low")
        up_done, relu_done, x2_high, x2_low = sem("up_done"), sem("relu_done"), sem("x2_high"), sem("x2_low")
        down_done, down_read, y_base = sem("down_done"), sem("down_read"), sem("y_base")

        wuq_v = wuq.rearrange("(g j p) c -> g p j c", p=P, j=4)
        wdq_v = wdq.rearrange("(j p) (g c) -> g p j c", p=P, c=512)
        out_v = out
        wo_nat = y

        def after(eng, s, value):
            if not isinstance(value, int) or value > 0:
                eng.wait_ge(s, value)

        def halves(v, swap):
            v = v.rearrange("p (h s d) -> p h s d", s=2, d=HD // 2)
            return v[:, :, ::-1, :] if swap else v

        def scale_of(t):
            g, j = divmod(t, 4)
            v = s_up[:, t, :] if g < 4 else s_dn[:, j, 8 * (g - 4):8 * (g - 4) + 8]
            return v.unsqueeze(2).broadcast_to([P, 8, QB])

        block = es.enter_context(nc.Block())

        def before(slots, s, itself=False):
            return sum(v < s or (itself and v == s) for v in slots)

        b_pieces = ((b_up3[:, 0:512], b_up_in[:, 0:512], 4), (b_up3[:, 512:], b_up_in[:, 512:], 4),
                    (b_dn3[:], b_dn_in, 5))

        def tiles_to_dequantise(s):
            t = s - LAG + DEQ_LEAD
            return range(DEQ_LEAD - LAG + 2) if s == 1 else range(t, t + 1) if 1 < s and t < SLOTS else ()

        QTURN_AT = tuple(v + R_QTURN for v in BASE)
        PV_AT = tuple(v + R_PV for v in BASE)
        PROJ_AT = tuple(v + R_PROJ for v in BASE)

        @block.sync
        def _(sp):
            def load_batch(A, c):
                after(sp, x1_ready, 4 * A - 3 + c)
                sp.dma_start(xt[:, c, :], x[4 * A + c]).then_inc(x_in[c], 16)
                after(sp, heads_out, 4 * A - 3 + c)
                sp.dma_start(kvt[:, c, :], ctx[4 * A + c]).then_inc(kv_in[c], 16)

            def load_group(g):
                if g >= 4:
                    after(sp, w_turned, 4 * (g - 3))
                src = wuq_v[g] if g < 4 else wdq_v[g - 4]
                sp.dma_start(stage_i[:, g % 4], src).then_inc(wq_in[g % 4], 16)

            sp.dma_start(s_up[:], wus.rearrange("(c p) b -> p c b", p=P)).then_inc(scales_in, 16)
            sp.dma_start(s_dn[:], wds.rearrange("(c p) b -> p c b", p=P)).then_inc(scales_in, 16)
            load_batch(0, 0)
            for src, dst in ((kw, kw_bc), (qw, qw_bc)):
                n = src.shape[0]
                sp.dma_start(dst, src.rearrange("(a n) -> a n", a=1).broadcast_to([P, n])).then_inc(norm_w_in, 16)
            load_group(0)
            for i in range(3):
                sp.dma_start(b_up_in[R * i:R * i + R], wub).then_inc(b_in, 16)
                sp.dma_start(b_dn_in[R * i:R * i + R], wdb).then_inc(b_in, 16)
            sp.dma_start(wo_raw, wo.rearrange("(j p) c -> p j c", p=P)).then_inc(wout_in, 16)
            load_batch(0, 1)
            load_group(1)
            load_batch(0, 2)
            load_group(2)
            load_group(3)
            load_batch(0, 3)
            sp.dma_start(bd_bc[:], bd.rearrange("(a n) -> a n", a=1).broadcast_to([P, C])).then_inc(down_bias_in, 16)
            for g in range(4, 8):
                load_group(g)
            with sp.Fori(0, NBLK - 1) as i:
                for c in range(BPB):
                    load_batch(i + 1, c)

        @block.gpsimd
        def _(pool):
            pool.dma_start(b_up_flat, wub.rearrange("r (a c) -> (r a) c", a=P // R)).then_inc(b_flat_in, 16)
            pool.dma_start(b_dn_flat, wdb.rearrange("r (a c) -> (r a) c", a=P // R)).then_inc(b_flat_in, 16)
            pool.memset(minus_half[:], -0.5).then_inc(pool_consts, 1)

            def rotary_tables(*tables):
                for dst, w, tab, swap in tables:
                    n = w.shape[1] // HD
                    pool.tensor_tensor(halves(dst[:], False), halves(w, swap),
                                       tab.rearrange("p (s d) -> p s d", s=2).unsqueeze(1).broadcast_to([P, n, 2, HD // 2]),
                                       ALU.mult).then_inc(tables_ready, 1)

            def dequant(t):
                g, j = divmod(t, 4)
                v, vi = stage[:, g % 4, j, :], stage_i[:, g % 4, j, :]
                pool.wait_ge(wq_in[g % 4], 16 * (g // 4 + 1))
                pool.tensor_scalar(v, vi, -7.5, 1.0, ALU.add, ALU.mult).then_inc(deq_g1, 1)
                pool.wait_ge(deq_g1, t + 1 - len([u for u in DVE_TILES if u < t]))
                pool.wait_ge(scales_ready, 2)
                pool.tensor_tensor(v.rearrange("p (b c) -> p b c", c=QB), v.rearrange("p (b c) -> p b c", c=QB),
                                   scale_of(t), ALU.mult).then_inc(deq_g, 1)

            def probs_and_cosines(A, s):
                for c in range(BPB):
                    r = s - BASE[c]
                    n = 4 * A + c + 1
                    p = c % 2
                    if r in R_PROBS:
                        m = r - R_PROBS[0]
                        pool.wait_ge(inv_sums, 4 * (n - 1) + m + 1)
                        pool.tensor_tensor(pr[:, m], pr[:, m],
                                           rinv[:, p, 4 * m:4 * m + 4].unsqueeze(2).broadcast_to([P, NG, P]),
                                           ALU.mult).then_inc(probs, 1)
                for c in range(BPB):
                    r = s - BASE[c]
                    n = 4 * A + c + 1
                    if r == R_CENTRE:
                        pool.wait_ge(x_centred, n)
                        pool.tensor_tensor(t_cos[:], xc[:], cw[:], ALU.mult).then_inc(q_cos, 1)

            def attention(A, s):
                for c in range(BPB):
                    r = s - BASE[c]
                    n = 4 * A + c + 1
                    p = c % 2
                    if r == R_STATS:
                        pool.wait_ge(kv_in[c], 16 * A + 16)
                        kv = kvt[:, c, :]
                        after(pool, k_low, n - 1)
                        after(pool, k_high, n - 1)
                        pool.tensor_tensor(k_cos[:], kv, cwk[:], ALU.mult).then_inc(k_parts, 1)
                        pool.tensor_tensor(halves(k_sin[:], False), halves(kv, True), halves(swk[:], False),
                                           ALU.mult).then_inc(k_parts, 1)
                        pool.wait_ge(k_parts, 2 * n)
                        pool.tensor_tensor(k_sum[:], k_cos[:], k_sin[:], ALU.add).then_inc(k_summed, 1)
                        pool.wait_ge(norm_args, 2 * n)
                        pool.tensor_tensor(inv[:, p, :], arg[:, p, :], minus_half[:], ALU.pow).then_inc(norms, 1)
                        pool.wait_ge(norms, n)
                        pool.wait_ge(k_summed, n)
                        pool.tensor_tensor(k[:], k_sum[:], inv[:, p, 1:2].broadcast_to([P, CK]), ALU.mult).then_inc(k_ready, 1)
                    if r == R_X1:
                        pool.wait_ge(arg2_ready, n)
                        pool.tensor_tensor(inv2[:, p:p + 1], arg2[:, p:p + 1], minus_half[:, 0:1],
                                           ALU.pow).then_inc(norm2, 1)

            def residual(F, c):
                pool.wait_ge(x1_ready, 4 * F + c + 1)
                pool.wait_ge(y_free[c], 16 * F + 16)
                pool.tensor_tensor(y[:, c, :], x1[:, c, :], bd_bc[:], ALU.add).then_inc(y_base, 1)

            pool.wait_ge(norm_w_in, 16 * 2)
            pool.wait_ge(consts_in, 16)
            rotary_tables((cwk, kw_bc, cos_s, False), (swk, kw_bc, sin_s, True))
            pool.wait_ge(tables_ready, 2)
            pool.wait_ge(tops_ready, 7)
            pool.partition_all_reduce(tops_all[:], tops[:], P, bass.bass_isa.ReduceOp.max).then_inc(tops_reduced, 1)
            attention(0, 0)
            rotary_tables((cw, qw_bc, cos_s, False), (sw, qw_bc, sin_s, True))
            pool.wait_ge(tables_ready, 4)
            for s in range(1, SLOTS + LAG):
                probs_and_cosines(0, s)
                if s == 1:
                    attention(0, s)
                for t in tiles_to_dequantise(s):
                    if t not in DVE_TILES:
                        dequant(t)
                if s > 1:
                    attention(0, s)
            pool.wait_ge(down_bias_in, 16)
            with pool.Fori(0, NBLK - 1) as i:
                for s in range(SLOTS):
                    probs_and_cosines(i + 1, s)
                    attention(i + 1, s)
                    if s in RESIDUAL_AT:
                        residual(i, RESIDUAL_AT.index(s))
            for c in range(BPB):
                residual(NBLK - 1, c)

        @block.scalar
        def _(act):
            act.dma_start(tabs[:], tabs_d).then_inc(consts_in, 16)
            act.dma_start(a_nat[:, 0:KC * R].rearrange("p (c r) -> p c r", r=R),
                          wua.rearrange("(c p) r -> p c r", p=P)).then_inc(scales_in, 16)
            act.dma_start(a_nat[:, KC * R:].rearrange("p (c r) -> p c r", r=R),
                          wda.rearrange("(c p) r -> p c r", p=P)).then_inc(scales_in, 16)
            act.dma_start(b_nat[:], bu.rearrange("(c p) -> c p", p=P)).then_inc(scales_in, 16)

            def order_wout():
                act.wait_ge(wout_in, 16)
                for j in range(KC):
                    act.activation(wo_nat[:, j, :].rearrange("p (n g d) -> p n g d", g=NG, d=HD),
                                   wo_raw[:, j, :].rearrange("p (g n d) -> p n g d", g=NG, d=HD),
                                   ACT.Copy).then_inc(wo_ordered, 1)

            def wout_high(m):
                act.wait_ge(wo_turned, m + 1)
                act.activation(wo_hi[:, m, :], tb[m % 2][:], ACT.Copy).then_inc(wo_high, 1)

            def lora_high():
                act.wait_ge(scale_steps, SCALE_STEPS)
                for cols, chunks, kx in ((slice(0, KC * R), slice(0, KC), 2), (slice(KC * R, None), slice(KC, None), 3)):
                    src = a_nat[:, cols].rearrange("p (c r) -> p c r", r=R)
                    act.activation(a_parts[:, chunks, 0:3:2, :],
                                   src.unsqueeze(2).broadcast_to([P, src.shape[1], 2, R]),
                                   ACT.Identity, scale=kap[:, kx:kx + 1]).then_inc(a_high, 1)
                act.wait_ge(b_in, 16 * 6)
                for dst, src, kx in b_pieces:
                    act.activation(dst, src, ACT.Identity, scale=kap[0:R3, kx:kx + 1]).then_inc(b_high, 1)

            def lora_copy():
                for i, dst in enumerate((a_up3[:], a_dn3[:, 0:1024], a_dn3[:, 1024:2048])):
                    n = 1024 if i else 512
                    act.wait_ge(a_turned, i + 1)
                    act.activation(dst, ff[i % 2][0:R3, :].bitcast(F16)[:, 0:n], ACT.Copy).then_inc(a_copied, 1)

            def weights(s):
                act.wait_ge(w_turned, s + 1)
                dst = wu_hi[:, s % 4, 512 * (s // 4):512 * (s // 4) + 512] if s < 16 else wd_hi[:, s - 16, :]
                act.activation(dst, ff[s % 2][:], ACT.Copy).then_inc(w_high, 1)

            def take_turned(A, s):
                for c in range(BPB):
                    r = s - BASE[c]
                    n = 4 * A + c + 1
                    if r == R_QTAKE[0]:
                        act.wait_ge(q_turned, 2 * n - 1)
                        act.activation(qT[:, 0:8].rearrange("p h t -> p (h t)"), prb16[0:HD3], ACT.Copy).then_inc(q_taken0, 1)
                    if r == R_KTAKE:
                        act.wait_ge(k_turned, n)
                        act.activation(kT[:].rearrange("p g t -> p (g t)"), pvb16[0:HD3, 0:NG * P], ACT.Copy).then_inc(k_taken, 1)

            def split_queries(A, s):
                for c in range(BPB):
                    r = s - BASE[c]
                    n = 4 * A + c + 1
                    if r == R_QSPLIT:
                        act.wait_ge(q_ready, n)
                        after(act, q_turned, 2 * (n - 1))
                        act.activation(q3[:, :, 0:3:2, :], q[:].rearrange("p (h d) -> p h d", d=HD).unsqueeze(2)
                                       .broadcast_to([P, NN * NG, 2, HD]), ACT.Copy).then_inc(q_high, 1)

            def split_heads_out(A, s):
                for c in range(BPB):
                    r = s - BASE[c]
                    n = 4 * A + c + 1
                    if r == R_PV:
                        act.wait_ge(heads_out, n)
                        act.activation(oT_hi[:].rearrange("p n t -> p (n t)"), pvb[:], ACT.Copy).then_inc(o_high, 1)

            def exponentials(A, s):
                for c in range(BPB):
                    r = s - BASE[c]
                    n = 4 * A + c + 1
                    p = c % 2
                    if r in R_EXP:
                        m = r - R_EXP[0]
                        act.wait_ge(row_max, 4 * (n - 1) + m + 1)
                        for g in range(NG):
                            j = 4 * m + g
                            last = act.activation(pr[:, m, g, :], pr[:, m, g, :], ACT.Exp,
                                                  bias=nmax[:, p, j:j + 1], scale=-1.0,
                                                  accum_out=rsum[:, p, j:j + 1])
                        last.then_inc(exps, 1)

            def attention(A, s):
                for c in range(BPB):
                    r = s - BASE[c]
                    n = 4 * A + c + 1
                    p = c % 2
                    if r == R_STATS:
                        act.wait_ge(kv_in[c], 16 * A + 16)
                        act.activation(sq_junk[:], kvt[:, c, :], ACT.Square, accum_out=ssq[:, p:p + 1]).then_inc(ctx_sq, 1)
                    if r == R_KSPLIT:
                        act.wait_ge(k_ready, n)
                        after(act, k_turned, n - 1)
                        act.activation(k3[:, :, 0:2, :], k[:].rearrange("p (g d) -> p g d", d=HD).unsqueeze(2)
                                       .broadcast_to([P, NG, 2, HD]), ACT.Copy).then_inc(k_high, 1)
                    if r in R_PT:
                        m = r - R_PT[0]
                        act.wait_ge(probs_turned, 4 * (n - 1) + m + 1)
                        act.activation(prT[:, :, m, :], tb[m % 2][:].rearrange("p (g t) -> p g t", g=NG),
                                       ACT.Copy).then_inc(probsT, 1)
                    if s == TURN2[c]:
                        act.wait_ge(xn2_turned, n)
                        act.activation(xnT_hi[:, :, P * c:P * c + P], prb[:].rearrange("p (k t) -> p k t", k=KC),
                                       ACT.Copy, scale=XN_SCALE).then_inc(xn_high, 1)
            def hidden(F, h):
                act.wait_ge(up_done, 16 * F + h + 1)
                if h >= 2:
                    act.wait_ge(x2_low, 16 * F + h - 1)
                act.activation(relu[:, h % 2, :], ff[h % 2][:], ACT.Relu, bias=b_up[:, h:h + 1],
                               scale=su[:]).then_inc(relu_done, 1)
                act.wait_ge(relu_done, 16 * F + h + 1)
                act.activation(x2_hi[:, h, :], relu[:, h % 2, :], ACT.Copy).then_inc(x2_high, 1)

            def store(F, t):
                act.wait_ge(down_read, 4 * F + 4 + t + 1)
                act.dma_start(out_v[4 * F + t], y[:, t, :]).then_inc(y_free[t], 16)

            def feed_forward(F, s):
                if 1 <= s <= 16:
                    hidden(F, s - 1)
                if s in (20, 24, 28):
                    store(F, (s - 20) // 4)

            for s in range(SLOTS + LAG + 1):
                if s == 2:
                    lora_copy()
                if s == 1:
                    lora_high()
                if s < SLOTS:
                    split_queries(0, s)
                    exponentials(0, s)
                if s > LAG:
                    weights(s - LAG - 1)
                if s < SLOTS:
                    take_turned(0, s)
                    split_heads_out(0, s)
                    attention(0, s)
                if s == 0:
                    act.wait_ge(consts_in, 16)
                    act.activation(ident16[:], ident, ACT.Copy).then_inc(ident_cast, 1)
                if s == 2:
                    order_wout()
                if WOUT_AT < s <= WOUT_AT + NN:
                    wout_high(s - WOUT_AT - 1)
            act.wait_ge(bias_scaled, 1)
            with act.Fori(0, NBLK - 1) as i:
                for s in range(SLOTS):
                    take_turned(i + 1, s)
                    feed_forward(i, s)
                    split_heads_out(i + 1, s)
                    split_queries(i + 1, s)
                    attention(i + 1, s)
                    exponentials(i + 1, s)
                store(i, 3)
            for s in range(SLOTS):
                feed_forward(NBLK - 1, s)
            store(NBLK - 1, 3)
            for t in range(BPB):
                act.wait_ge(y_free[t], 16 * NBLK + 16)

        @block.tensor
        def _(pe):
            def turn(dst, src, **kw):
                return pe.matmul(dst, src, ident[0:src.shape[0], 0:src.shape[0]], is_transpose=True, **kw)

            def wout_turn(m):
                if m == 0:
                    pe.wait_ge(consts_in, 16)
                    pe.wait_ge(wo_ordered, KC)
                if m >= 2:
                    pe.wait_ge(wo_low, m - 1)
                for j in range(KC):
                    last = turn(tb[m % 2][:, P * j:P * j + P], wo_nat[:, j, P * m:P * m + P], start=True, stop=True)
                last.then_inc(wo_turned, 1)

            def lora_turn():
                pe.wait_ge(ident_cast, 1)
                pe.wait_ge(a_high, 2)
                pe.wait_ge(a_low, 2)
                for i, chunks in enumerate((range(0, 4), range(4, 12), range(12, 20))):
                    if i == 2:
                        pe.wait_ge(a_copied, 1)
                    for j, b in enumerate(chunks):
                        last = pe.transpose(ff[i % 2][0:R3, 64 * j:64 * j + 64].bitcast(F16),
                                            a_parts[:, b].rearrange("p k r -> p (k r)"), ident16[:])
                    last.then_inc(a_turned, 1)

            def weights(s):
                if s < 2:
                    pe.wait_ge(a_copied, 3)
                elif s < 30:
                    pe.wait_ge(w_low, s - 1)
                else:
                    pe.wait_ge(down_read, s - 29)
                g, j = divmod(s, 4)
                if s in (0, 4):
                    pe.wait_ge(b_high, 1 if s == 0 else 3)
                    pe.wait_ge(b_low, 1 if s == 0 else 3)
                if s < 16:
                    a, b = a_up3[:, P * j:P * j + P], b_up3[:, 512 * g:512 * g + 512]
                else:
                    a, b = a_dn3[:, P * (s - 16):P * (s - 16) + P], b_dn3[:]
                lora = pe.matmul(ff[s % 2][:], a, b, start=True, stop=False, skip_group_check=True)
                if 8 <= s < 8 + BPB:
                    lora.then_inc(y_free[s - 8], 16)
                if j == 0:
                    by_dve = len([u for u in DVE_TILES if u < 4 * g + 4])
                    pe.wait_ge(deq_v, by_dve)
                    pe.wait_ge(deq_g, 4 * g + 4 - by_dve)
                for t in range(4):
                    last = turn(ff[s % 2][:, P * t:P * t + P], stage[:, g % 4, t, P * j:P * j + P],
                                start=False, stop=(t == 3), skip_group_check=True)
                last.then_inc(w_turned, 1)

            def turn_queries(h0):
                for h in range(8):
                    last = pe.transpose(prb16[0:HD3, P * h:P * h + P], q3[:, h0 + h].rearrange("p a d -> p (a d)"), ident16[:])
                last.then_inc(q_turned, 1)

            def attention(A, s):
                for c in range(BPB):
                    r = s - BASE[c]
                    n = 4 * A + c + 1
                    if r in R_PT:
                        m = r - R_PT[0]
                        pe.wait_ge(probs, 4 * (n - 1) + m + 1)
                        if isinstance(A, int) and c == 0 and m < 2:
                            pe.wait_ge(wo_low, NN - 1 + m)
                        after(pe, probsT, 4 * (n - 1) + m - 1)
                        for g in range(NG):
                            last = turn(tb[m % 2][:, P * g:P * g + P], pr[:, m, g, :], start=True, stop=True)
                        last.then_inc(probs_turned, 1)
                for c in range(BPB):
                    r = s - BASE[c]
                    n = 4 * A + c + 1
                    if r == R_QTURN:
                        pe.wait_ge(q_high, n)
                        pe.wait_ge(q_low, n)
                        after(pe, x1_ready, 4 * A + before(PROJ_AT, s))
                        after(pe, xn_low, 4 * A + before(TURN2, s))
                        turn_queries(0)
                    if r == R_PV:
                        pe.wait_ge(probsT, 4 * n)
                        after(pe, o_low, n - 1)
                        for g in range(NG):
                            d = slice(HD * g, HD * g + HD)
                            last = pe.matmul(pvb[d, :], kvt[:, c, d], prT[:, g].rearrange("p n t -> p (n t)"),
                                             start=True, stop=True)
                        last.then_inc(heads_out, 1)
                    if r == R_PROJ:
                        pe.wait_ge(o_low, n)
                        after(pe, x1_ready, n - 1)
                        after(pe, xn_low, 4 * A + before(TURN2, s))
                        after(pe, q_taken1, 4 * A + before(QTURN_AT, s))
                        if isinstance(A, int) and c == 0:
                            pe.wait_ge(wo_low, NN)
                        terms = ((oT_hi, wo_hi), (oT_lo, wo_hi), (oT_hi, wo_lo))
                        for i, (a, b) in enumerate(terms):
                            for m in range(NN):
                                last = pe.matmul(prb[:], a[:, m, :], b[:, m, :],
                                                 start=(i == 0 and m == 0), stop=(i == 2 and m == NN - 1))
                        last.then_inc(projected, 1)
                    if s == TURN2[c]:
                        pe.wait_ge(xn2_ready, n)
                        after(pe, x1_ready, 4 * A + before(PROJ_AT, s))
                        after(pe, xn_low, n - 1)
                        after(pe, q_taken1, 4 * A + before(QTURN_AT, s))
                        for m in range(KC):
                            last = turn(prb[:, P * m:P * m + P], xn2[:, c % 2, P * m:P * m + P], start=True, stop=True)
                        last.then_inc(xn2_turned, 1)

            def attention_end(A, s):
                for c in range(BPB):
                    r = s - BASE[c]
                    n = 4 * A + c + 1
                    if r in R_SCORES:
                        m = r - R_SCORES[0]
                        if m == 0:
                            pe.wait_ge(q_taken0, n)
                            pe.wait_ge(k_taken, n)
                            if isinstance(A, int) and c == 0:
                                pe.wait_ge(bias_scaled, 1)
                        if m == 2:
                            pe.wait_ge(q_taken1, n)
                        after(pe, masked, 4 * (n - 1) + m - 1)
                        for g in range(NG):
                            last = pe.matmul(sbk[m % 2][:, P * g:P * g + P], qT[:, 4 * m + g, :], kT[:, g, :],
                                             start=True, stop=True)
                        last.then_inc(scores, 1)
                for c in range(BPB):
                    r = s - BASE[c]
                    n = 4 * A + c + 1
                    if r == R_KTURN:
                        pe.wait_ge(k_high, n)
                        pe.wait_ge(k_low, n)
                        if isinstance(A, int) and c == 0:
                            pe.wait_ge(ident_cast, 1)
                        after(pe, o_low, 4 * A + before(PV_AT, s))
                        for g in range(NG):
                            last = pe.transpose(pvb16[0:HD3, P * g:P * g + P], k3[:, g].rearrange("p a d -> p (a d)"), ident16[:])
                        last.then_inc(k_turned, 1)
                    if r == R_QTURN:
                        pe.wait_ge(q_taken0, n)
                        turn_queries(8)

            def feed_forward(F, s):
                if s < HC:
                    if s == 0:
                        pe.wait_ge(xn_low, 4 * F + 4)
                    if s < 2:
                        pe.wait_ge(down_read, 4 * F + 3 + s)
                    else:
                        pe.wait_ge(relu_done, 16 * F + s - 1)
                    terms = ((wu_hi, xnT_hi), (wu_hi, xnT_lo), (wu_lo, xnT_hi))
                    for m in range(KC):
                        for i, (a, b) in enumerate(terms):
                            last = pe.matmul(ff[s % 2][:], a[:, m, P * s:P * s + P], b[:, m, :],
                                             start=(m == 0 and i == 0), stop=(m == KC - 1 and i == 2))
                    last.then_inc(up_done, 1)
                else:
                    t, part = divmod(s - HC, 4)
                    if part == 0:
                        if t < 2:
                            pe.wait_ge(relu_done, 16 * F + 15 + t)
                        else:
                            pe.wait_ge(down_read, 4 * F + 4 + t - 1)
                    terms = ((x2_hi, wd_hi), (x2_lo, wd_hi), (x2_hi, wd_lo))
                    for h in range(4 * part, 4 * part + 4):
                        if t == 0:
                            pe.wait_ge(x2_low, 16 * F + h + 1)
                        for i, (a, b) in enumerate(terms):
                            last = pe.matmul(ff[t % 2][:], a[:, h, P * t:P * t + P], b[:, h, :],
                                             start=(h == 0 and i == 0), stop=(h == HC - 1 and i == 2))
                    if part == 3:
                        last.then_inc(down_done, 1)

            for s in range(SLOTS + LAG):
                if s < SLOTS:
                    attention(0, s)
                if s == 0:
                    pe.wait_ge(consts_in, 16)
                    pe.wait_ge(scales_in, 16 * 5)
                    turn(sbk[0][:, 0:HC], b_nat[:], start=True, stop=True).then_inc(b_turned, 1)
                if s == 1:
                    lora_turn()
                if s >= LAG:
                    weights(s - LAG)
                if WOUT_AT <= s < WOUT_AT + NN:
                    wout_turn(s - WOUT_AT)
                if s < SLOTS:
                    attention_end(0, s)
            with pe.Fori(0, NBLK - 1) as i:
                for s in range(SLOTS):
                    attention(i + 1, s)
                    feed_forward(i, s)
                    attention_end(i + 1, s)
            for s in range(SLOTS):
                feed_forward(NBLK - 1, s)

        @block.vector
        def _(dve):
            step = [0]

            def link(ins, wait=True):
                step[0] += 1
                ins.then_inc(scale_steps, 1)
                if wait:
                    dve.wait_ge(scale_steps, step[0])

            def norm_scales():
                done = [0]

                def link(ins, wait=True):
                    done[0] += 1
                    ins.then_inc(norm_scale_steps, 1)
                    if wait:
                        dve.wait_ge(norm_scale_steps, done[0])
                dve.wait_ge(norm_w_in, 16 * 2)
                for j, w in enumerate((qw_bc, kw_bc)):
                    link(dve.tensor_reduce(wmax[:, j:j + 1], w, AXX, ALU.max, apply_absolute_value=True), wait=(j == 1))
                link(dve.tensor_scalar(wmax[:], wmax[:], 1e-12, None, ALU.add))
                link(dve.tensor_scalar(wpow2[:].bitcast(I32), wmax[:].bitcast(I32), 0x7F800000, None, ALU.bitwise_and))
                link(dve.tensor_tensor(wsq[:], wpow2[:], wpow2[:], ALU.mult))
                for j, (unit, mul, add) in enumerate(((Q_TOP, 1.0 + EPS, EPS * EPS), (K_TOP, 1.0 / CK, EPS))):
                    link(dve.tensor_scalar(arg_mul[:, j:j + 1], wsq[:, j:j + 1], mul / unit ** 2, None, ALU.mult), wait=False)
                    link(dve.tensor_scalar(arg_add[:, j:j + 1], wsq[:, j:j + 1], add / unit ** 2, None, ALU.mult), wait=False)
                link(dve.tensor_scalar(score_scale[:], wpow2[:, 0:1], wpow2[:, 1:2], -SC / (Q_TOP * K_TOP), ALU.mult, ALU.mult))

            def find_tops():
                dve.memset(tops[:], 0.0).then_inc(tops_zero, 1)
                dve.wait_ge(tops_zero, 1)
                dve.wait_ge(scales_in, 16 * 5)
                dve.wait_ge(b_flat_in, 16 * 2)
                for j, v in enumerate((s_up[:].rearrange("p a b -> p (a b)"), s_dn[:].rearrange("p a b -> p (a b)"),
                                       a_nat[:, 0:KC * R], a_nat[:, KC * R:], b_up_flat, b_dn_flat, b_nat[:])):
                    dve.tensor_reduce(tops[0:v.shape[0], j:j + 1], v, AXX, ALU.max,
                                      apply_absolute_value=True).then_inc(tops_ready, 1)

            def find_scales():
                dve.wait_ge(tops_reduced, 1)
                lora, deq, wtop, wpow, ytop, atop, apow = (tmp[:, 2 * i:2 * i + 2] for i in range(7))
                link(dve.tensor_tensor(lora, tops_all[:, 2:4], tops_all[:, 4:6], ALU.mult), wait=False)
                link(dve.tensor_scalar(deq, tops_all[:, 0:2], 7.5, 1e-30, ALU.mult, ALU.add), wait=False)
                link(dve.tensor_scalar(atop, tops_all[:, 2:4], 1e-30, None, ALU.add))
                link(dve.scalar_tensor_tensor(wtop, lora, float(R), deq, ALU.mult, ALU.add))
                link(dve.scalar_tensor_tensor(ytop[:, 0:1], wtop[:, 0:1], float(C), tops_all[:, 6:7], ALU.mult, ALU.add))
                for dst, src, wait in ((wpow, wtop, False), (apow, atop, False), (ytop[:, 1:2], ytop[:, 0:1], True)):
                    link(dve.tensor_scalar(dst.bitcast(I32), src.bitcast(I32), 0x7F800000, None, ALU.bitwise_and), wait)
                link(dve.reciprocal(kap[:, 0:2], wpow), wait=False)
                link(dve.reciprocal(kap[:, 2:4], apow), wait=False)
                link(dve.reciprocal(kap[:, 6:7], ytop[:, 1:2]))
                link(dve.tensor_scalar(kap[:, 0:2], kap[:, 0:2], W_TOP, None, ALU.mult), wait=False)
                link(dve.tensor_scalar(kap[:, 2:4], kap[:, 2:4], A_TOP, None, ALU.mult), wait=False)
                link(dve.tensor_scalar(kap[:, 6:7], kap[:, 6:7], X2_TOP, None, ALU.mult))
                link(dve.scalar_tensor_tensor(kap[:, 4:6], kap[:, 0:2], 1.0 / A_TOP, apow, ALU.mult, ALU.mult), wait=False)
                link(dve.tensor_scalar(su[:], wpow[:, 0:1], kap[:, 6:7], 1.0 / (W_TOP * XN_SCALE), ALU.mult, ALU.mult), wait=False)
                link(dve.tensor_scalar(sd[:], wpow[:, 1:2], ytop[:, 1:2], 1.0 / (W_TOP * X2_TOP), ALU.mult, ALU.mult), wait=False)
                for v, kx in ((s_up[:], kap[:, 0:1]), (s_dn[:], kap[:, 1:2])):
                    dve.tensor_scalar(v, v, kx, None, ALU.mult).then_inc(scales_ready, 1)
                assert step[0] == SCALE_STEPS
                dve.wait_ge(scales_ready, 2)

            def lora_a_low():
                dve.wait_ge(a_high, 2)
                for cols, chunks, kx in ((slice(0, KC * R), slice(0, KC), 2), (slice(KC * R, None), slice(KC, None), 3)):
                    dve.scalar_tensor_tensor(a_parts[:, chunks, 1, :], a_nat[:, cols].rearrange("p (c r) -> p c r", r=R),
                                             kap[:, kx:kx + 1], a_parts[:, chunks, 0, :],
                                             ALU.mult, ALU.subtract).then_inc(a_low, 1)

            def lora_b_low(pieces):
                rows = slice(2 * R, R3)
                for i, (dst, src, kx) in tuple(enumerate(b_pieces))[pieces]:
                    dve.wait_ge(b_high, i + 1)
                    dve.scalar_tensor_tensor(dst[rows], src[rows], kap[rows, kx:kx + 1], dst[rows],
                                             ALU.mult, ALU.subtract).then_inc(b_low, 1)

            def wout_low(m):
                dve.wait_ge(wo_high, m + 1)
                dve.tensor_tensor(wo_lo[:, m, :], tb[m % 2][:], wo_hi[:, m, :].bitcast(F32),
                                  ALU.subtract).then_inc(wo_low, 1)

            def dequant(t):
                g, j = divmod(t, 4)
                dve.wait_ge(wq_in[g % 4], 16 * (g // 4 + 1))
                dve.scalar_tensor_tensor(stage[:, g % 4, j, :].rearrange("p (b c) -> p b c", c=QB),
                                         stage_i[:, g % 4, j, :].rearrange("p (b c) -> p b c", c=QB), -7.5,
                                         scale_of(t), ALU.add, ALU.mult).then_inc(deq_v, 1)

            def weights(s):
                dve.wait_ge(w_high, s + 1)
                cols = slice(512 * (s // 4), 512 * (s // 4) + 512)
                hi, lo = ((wu_hi[:, s % 4, cols], wu_lo[:, s % 4, cols]) if s < 16 else
                          (wd_hi[:, s - 16, :], wd_lo[:, s - 16, :]))
                dve.tensor_tensor(lo, ff[s % 2][:], hi, ALU.subtract).then_inc(w_low if s < 28 else down_read, 1)

            def sums_and_rope(A, s):
                for c in range(BPB):
                    r = s - BASE[c]
                    n = 4 * A + c + 1
                    p = c % 2
                    if r in R_PROBS:
                        m = r - R_PROBS[0]
                        dve.wait_ge(exps, 4 * (n - 1) + m + 1)
                        dve.reciprocal(rinv[:, p, 4 * m:4 * m + 4], rsum[:, p, 4 * m:4 * m + 4]).then_inc(inv_sums, 1)
                for c in range(BPB):
                    r = s - BASE[c]
                    n = 4 * A + c + 1
                    if r == R_ROPE:
                        dve.wait_ge(q_cos, n)
                        dve.wait_ge(q_sin, n)
                        after(dve, q_high, n - 1)
                        dve.tensor_tensor(q[:].rearrange("p (n g d) -> p g n d", g=NG, d=HD),
                                          t_cos[:].rearrange("p (g n d) -> p g n d", g=NG, d=HD),
                                          t_sin[:].rearrange("p (g n d) -> p g n d", g=NG, d=HD),
                                          ALU.add).then_inc(q_ready, 1)

            def attention_early(A, s):
                for c in range(BPB):
                    r = s - BASE[c]
                    n = 4 * A + c + 1
                    p = c % 2
                    if r == R_STATS:
                        dve.wait_ge(x_in[c], 16 * A + 16)
                        dve.bn_stats(stats[:, p, :], xt[:, c, :]).then_inc(x_stats, 1)
                    if r == R_CENTRE:
                        dve.wait_ge(norms, n)
                        after(dve, q_cos, n - 1)
                        dve.tensor_scalar(xc[:], xt[:, c, :], mv[:, p, 0:1], inv[:, p, 0:1],
                                          ALU.subtract, ALU.mult).then_inc(x_centred, 1)
                        dve.wait_ge(x_centred, n)
                        if isinstance(A, int) and c == 0:
                            dve.wait_ge(tables_ready, 4)
                        dve.tensor_tensor(halves(t_sin[:], False), halves(xc[:], True), halves(sw[:], False),
                                          ALU.mult).then_inc(q_sin, 1)
                    if r == R_X1:
                        dve.wait_ge(projected, n)
                        after(dve, y_base, n - 4)
                        dve.tensor_tensor(x1[:, c, :], prb[:], xt[:, c, :], ALU.add).then_inc(x1_ready, 1)
                        dve.wait_ge(x1_ready, n)
                        dve.bn_stats(stats2[:, p, :], x1[:, c, :]).then_inc(x1_stats, 1)
                        dve.wait_ge(x1_stats, n)
                        dve.memset(spare[:], 0.0)
                        dve.bn_aggr(mv2[:, p, :], stats2[:, p, :]).then_inc(x1_moments, 1)
                        dve.wait_ge(x1_moments, n)
                        dve.tensor_scalar(arg2[:, p:p + 1], mv2[:, p, 1:2], EPS, None, ALU.add).then_inc(arg2_ready, 1)
                for c in range(BPB):
                    r = s - BASE[c]
                    n = 4 * A + c + 1
                    p = c % 2
                    if r in R_MASK:
                        m = r - R_MASK[0]
                        dve.wait_ge(scores, 4 * (n - 1) + m + 1)
                        dve.scalar_tensor_tensor(pr[:, m], sbk[m % 2][:].rearrange("p (g t) -> p g t", g=NG), score_scale[:],
                                                 mask.unsqueeze(1).broadcast_to([P, NG, P]),
                                                 ALU.mult, ALU.add).then_inc(masked, 1)
                        dve.wait_ge(masked, 4 * (n - 1) + m + 1)
                        dve.tensor_reduce(nmax[:, p, 4 * m:4 * m + 4], pr[:, m], AXX, ALU.min).then_inc(row_max, 1)
                for c in range(BPB):
                    r = s - BASE[c]
                    n = 4 * A + c + 1
                    if r == R_QTAKE[1]:
                        dve.wait_ge(q_turned, 2 * n)
                        dve.tensor_scalar(qT[:, 8:16].rearrange("p h t -> p (h t)"), prb16[0:HD3], 1.0, None,
                                          ALU.mult).then_inc(q_taken1, 1)
                    if r == R_QSPLIT:
                        dve.wait_ge(q_high, n)
                        dve.tensor_tensor(q3[:, :, 1, :], q[:].rearrange("p (h d) -> p h d", d=HD), q3[:, :, 0, :],
                                          ALU.subtract).then_inc(q_low, 1)

            def attention_late(A, s):
                for c in range(BPB):
                    r = s - BASE[c]
                    n = 4 * A + c + 1
                    p = c % 2
                    if r == R_STATS:
                        dve.wait_ge(ctx_sq, n)
                        dve.wait_ge(x_stats, n)
                        dve.tensor_scalar(arg[:, p, 1:2], ssq[:, p:p + 1], arg_mul[:, 1:2], arg_add[:, 1:2],
                                          ALU.mult, ALU.add).then_inc(norm_args, 1)
                        dve.bn_aggr(mv[:, p, :], stats[:, p, :]).then_inc(x_moments, 1)
                        dve.wait_ge(x_moments, n)
                        dve.tensor_scalar(arg[:, p, 0:1], mv[:, p, 1:2], arg_mul[:, 0:1], arg_add[:, 0:1],
                                          ALU.mult, ALU.add).then_inc(norm_args, 1)
                    if r == R_KSPLIT:
                        dve.wait_ge(k_high, n)
                        after(dve, k_turned, n - 1)
                        dve.tensor_tensor(k3[:, :, 2, :], k[:].rearrange("p (g d) -> p g d", d=HD), k3[:, :, 0, :],
                                          ALU.subtract).then_inc(k_low, 1)
                    if r == R_PV:
                        dve.wait_ge(o_high, n)
                        dve.tensor_tensor(oT_lo[:].rearrange("p n t -> p (n t)"), pvb[:],
                                          oT_hi[:].rearrange("p n t -> p (n t)").bitcast(F32),
                                          ALU.subtract).then_inc(o_low, 1)
                    if r == R_NORM2:
                        dve.wait_ge(norm2, n)
                        after(dve, xn2_turned, n - 2)
                        dve.tensor_scalar(xn2[:, p, :], x1[:, c, :], mv2[:, p, 0:1], inv2[:, p:p + 1],
                                          ALU.subtract, ALU.mult).then_inc(xn2_ready, 1)
                    if s == TURN2[c]:
                        dve.wait_ge(xn_high, n)
                        dve.scalar_tensor_tensor(xnT_lo[:, :, P * c:P * c + P], prb[:].rearrange("p (k t) -> p k t", k=KC),
                                                 XN_SCALE, xnT_hi[:, :, P * c:P * c + P],
                                                 ALU.mult, ALU.subtract).then_inc(xn_low, 1)

            def result(F, t):
                dve.wait_ge(down_done, 4 * F + t + 1)
                dve.wait_ge(y_base, 4 * F + t + 1)
                dve.scalar_tensor_tensor(y[:, t, :], ff[t % 2][:], sd[:], y[:, t, :],
                                         ALU.mult, ALU.add).then_inc(down_read, 1)

            def x2_lows(F, s):
                if 1 <= s <= 16:
                    h = s - 1
                    dve.wait_ge(x2_high, 16 * F + h + 1)
                    dve.tensor_tensor(x2_lo[:, h, :], relu[:, h % 2, :], x2_hi[:, h, :], ALU.subtract).then_inc(x2_low, 1)

            for s in range(SLOTS + LAG + 2):
                if s < SLOTS:
                    sums_and_rope(0, s)
                if s == 1:
                    find_scales()
                    dequant(0)
                    lora_a_low()
                    dve.wait_ge(b_turned, 1)
                    dve.tensor_scalar(b_up[:], sbk[0][:, 0:HC], kap[:, 6:7], None, ALU.mult).then_inc(bias_scaled, 1)
                if s > LAG + 1:
                    weights(s - LAG - 2)
                for t in tiles_to_dequantise(s):
                    if t in DVE_TILES and t > 0:
                        dequant(t)
                if s < SLOTS:
                    attention_early(0, s)
                    if s == 0:
                        find_tops()
                        norm_scales()
                    attention_late(0, s)
                if s in (1, 2):
                    lora_b_low(slice(0, 1) if s == 1 else slice(1, 3))
                if WOUT_AT < s <= WOUT_AT + NN:
                    wout_low(s - WOUT_AT - 1)
            with dve.Fori(0, NBLK - 1) as i:
                for s in range(SLOTS):
                    if s in (20, 24, 28):
                        result(i, (s - 20) // 4)
                    sums_and_rope(i + 1, s)
                    attention_early(i + 1, s)
                    x2_lows(i, s)
                    attention_late(i + 1, s)
                result(i, 3)
            for s in range(SLOTS):
                if s in (20, 24, 28):
                    result(NBLK - 1, (s - 20) // 4)
                x2_lows(NBLK - 1, s)
            result(NBLK - 1, 3)


_INS = ["x", "ctx_512", "L0_xattn_q_norm_w", "L0_xattn_k_norm_w", "L0_xattn_w_out",
        "L0_ffn_w_up_q", "L0_ffn_w_up_scale", "L0_ffn_b_up", "L0_ffn_w_up_lora_a", "L0_ffn_w_up_lora_b",
        "L0_ffn_w_down_q", "L0_ffn_w_down_scale", "L0_ffn_b_down", "L0_ffn_w_down_lora_a", "L0_ffn_w_down_lora_b"]


def shape_tables(T=128, HD=32, theta=10000.0):
    f = np.float32
    inv_freq = f(1.0) / np.power(f(theta), np.arange(0, HD, 2, dtype=f) / f(HD)).astype(f)
    freqs = np.outer(np.arange(T, dtype=f), inv_freq).astype(f)
    emb = np.concatenate([freqs, freqs], -1)
    sin = np.sin(emb).astype(f)
    sin[:, :HD // 2] *= f(-1.0)
    causal = np.where(np.tril(np.ones((T, T), bool)), f(0), f(BIG)).astype(f)
    return {"tables": np.concatenate([np.eye(T, dtype=f), causal, np.cos(emb).astype(f), sin], 1)}


def kernel(**inputs):
    import concourse.bacc as _bacc
    from concourse import mybir as _mybir
    from concourse.bass_utils import run_bass_kernel_spmd as _run

    nc = _bacc.Bacc("TRN2", target_bir_lowering=False, num_devices=1)
    arrays, args = {}, []
    for name, a in [(n, inputs[n]) for n in _INS] + list(shape_tables().items()):
        a = np.ascontiguousarray(a)
        arrays[f"in_{name}"] = a
        args.append(nc.dram_tensor(f"in_{name}", a.shape, _mybir.dt.from_np(a.dtype), kind="ExternalInput").ap())
    args.append(nc.dram_tensor("out_0", tuple(inputs["x"].shape), _mybir.dt.float32, kind="ExternalOutput").ap())
    build(nc, *args)
    r = _run(nc, [arrays], core_ids=[0])
    return r.results[0]["out_0"]
```
